# Optimizing a Trainium2 kernel written in Bass

```python
import numpy as np
import jax
import jax.numpy as jnp

def _softmax(x, axis=-1):
    return jax.nn.softmax(x, axis=axis)

def _gelu(x):
    return jax.nn.gelu(x, approximate=True)

def _silu(x):
    return jax.nn.silu(x)

def _sigmoid(x):
    return jax.nn.sigmoid(x)

def _layernorm(x, axis=-1, eps=1e-05):
    m = jnp.mean(x, axis=axis, keepdims=True)
    v = jnp.var(x, axis=axis, keepdims=True)
    return (x - m) / jnp.sqrt(v + eps)

def _scatter_add(tgt, idx, src, axis=0):
    return tgt.at[idx].add(src)

def _segment_sum(src, seg, n):
    return jax.ops.segment_sum(src, seg, n)
kernel_name = 'mk_macaron_d1_jaxref_r4_a51e5d'

def setup_inputs(seed: int=0):
    np.random.seed(seed)
    _w = jnp.asarray

    def _L0_attn_setup():
        import jax, jax.numpy as jnp
        import numpy as np
        from jax import lax
        D_MODEL = 256
        N_HEADS = 16
        HEAD_DIM = D_MODEL // N_HEADS
        B, S = (4, 512)
        EPS = 1e-05

        def _l2_normalize(v, eps=1e-12):
            v32 = v.astype(jnp.float32)
            n = jnp.sqrt(jnp.sum(v32 * v32, axis=-1, keepdims=True))
            return (v32 / jnp.maximum(n, eps)).astype(v.dtype)

        def _rmsnorm(x, w):
            x32 = x.astype(jnp.float32)
            rms = lax.rsqrt(jnp.mean(x32 * x32, axis=-1, keepdims=True) + EPS)
            return (x32 * rms).astype(x.dtype) * w
        if __name__ == '__main__':
            out = reference(**setup_inputs())
            print(out.shape)
        key = jax.random.key(seed)
        ks = jax.random.split(key, 8)
        sc = 1.0 / np.sqrt(D_MODEL)
        return {'x': jax.random.normal(ks[0], (B, S, D_MODEL), dtype=jnp.float32), 'Wq': jax.random.normal(ks[1], (D_MODEL, D_MODEL), dtype=jnp.float32) * sc, 'Wk': jax.random.normal(ks[2], (D_MODEL, D_MODEL), dtype=jnp.float32) * sc, 'Wv': jax.random.normal(ks[3], (D_MODEL, D_MODEL), dtype=jnp.float32) * sc, 'Wa': jax.random.normal(ks[4], (D_MODEL, N_HEADS), dtype=jnp.float32) * sc, 'ba': jnp.zeros((N_HEADS,), dtype=jnp.float32), 'Wb': jax.random.normal(ks[5], (D_MODEL, N_HEADS), dtype=jnp.float32) * sc, 'bb': jnp.zeros((N_HEADS,), dtype=jnp.float32), 'Wg': jax.random.normal(ks[6], (D_MODEL, D_MODEL), dtype=jnp.float32) * sc, 'Wo': jax.random.normal(ks[7], (D_MODEL, D_MODEL), dtype=jnp.float32) * sc, 'g_norm': jnp.ones((D_MODEL,), dtype=jnp.float32)}
    _L0_attn_in = _L0_attn_setup()

    def _L0_ffn_setup():
        import jax, jax.numpy as jnp
        import numpy as np
        SL, BS, HS = (512, 4, 256)
        FF = 1024
        E, RANK, TOPK = (8, 64, 2)
        key = jax.random.key(seed)
        ks = jax.random.split(key, 7)
        s = 0.02
        return {'x': jax.random.normal(ks[0], (SL, BS, HS), jnp.float32), 'expert_weights': jax.random.uniform(ks[1], (SL * BS, TOPK), jnp.float32), 'expert_indices': jax.random.randint(ks[2], (SL * BS, TOPK), 0, E).astype(jnp.int32), 'w1_A': jax.random.normal(ks[3], (E * RANK, HS), jnp.float32) * s, 'w1_B': jax.random.normal(ks[4], (E * RANK, FF), jnp.float32) * s, 'w2_A': jax.random.normal(ks[5], (E * RANK, FF), jnp.float32) * s, 'w2_B': jax.random.normal(ks[6], (E * RANK, HS), jnp.float32) * s}
    _L0_ffn_in = _L0_ffn_setup()
    _d = {'L0_attn_x': _L0_attn_in['x'], 'L0_attn_Wq': _L0_attn_in['Wq'], 'L0_attn_Wk': _L0_attn_in['Wk'], 'L0_attn_Wv': _L0_attn_in['Wv'], 'L0_attn_Wa': _L0_attn_in['Wa'], 'L0_attn_ba': _L0_attn_in['ba'], 'L0_attn_Wb': _L0_attn_in['Wb'], 'L0_attn_bb': _L0_attn_in['bb'], 'L0_attn_Wg': _L0_attn_in['Wg'], 'L0_attn_Wo': _L0_attn_in['Wo'], 'L0_attn_g_norm': _L0_attn_in['g_norm'], 'L0_ffn_expert_weights': _L0_ffn_in['expert_weights'], 'L0_ffn_expert_indices': _L0_ffn_in['expert_indices'], 'L0_ffn_w1_A': _L0_ffn_in['w1_A'], 'L0_ffn_w1_B': _L0_ffn_in['w1_B'], 'L0_ffn_w2_A': _L0_ffn_in['w2_A'], 'L0_ffn_w2_B': _L0_ffn_in['w2_B']}
    _x0 = _d['L0_attn_x']
    _d['L0_attn_x'] = jax.random.normal(jax.random.fold_in(jax.random.key(seed), 1), (8, 1024, 256), dtype=_x0.dtype)
    del _x0
    return _d

def reference(L0_attn_x, L0_attn_Wq, L0_attn_Wk, L0_attn_Wv, L0_attn_Wa, L0_attn_ba, L0_attn_Wb, L0_attn_bb, L0_attn_Wg, L0_attn_Wo, L0_attn_g_norm, L0_ffn_expert_weights, L0_ffn_expert_indices, L0_ffn_w1_A, L0_ffn_w1_B, L0_ffn_w2_A, L0_ffn_w2_B):

    def _L0_attn_ref(x, Wq, Wk, Wv, Wa, ba, Wb, bb, Wg, Wo, g_norm):
        import jax, jax.numpy as jnp
        import numpy as np
        from jax import lax
        D_MODEL = 256
        N_HEADS = 16
        HEAD_DIM = D_MODEL // N_HEADS
        B, S = (4, 512)
        EPS = 1e-05

        def _l2_normalize(v, eps=1e-12):
            v32 = v.astype(jnp.float32)
            n = jnp.sqrt(jnp.sum(v32 * v32, axis=-1, keepdims=True))
            return (v32 / jnp.maximum(n, eps)).astype(v.dtype)

        def _rmsnorm(x, w):
            x32 = x.astype(jnp.float32)
            rms = lax.rsqrt(jnp.mean(x32 * x32, axis=-1, keepdims=True) + EPS)
            return (x32 * rms).astype(x.dtype) * w
        if __name__ == '__main__':
            out = reference(**setup_inputs())
            print(out.shape)
        batch, seq_len, d_model = x.shape
        H, hd = (N_HEADS, HEAD_DIM)
        residual_input = x
        q = (x @ Wq).reshape(batch, seq_len, H, hd)
        k = (x @ Wk).reshape(batch, seq_len, H, hd)
        v = (x @ Wv).reshape(batch, seq_len, H, hd)
        q = _l2_normalize(q)
        k = _l2_normalize(k)
        alpha = jax.nn.sigmoid(x @ Wa + ba)
        beta = jax.nn.sigmoid(x @ Wb + bb)
        qt = jnp.moveaxis(q, 1, 0)
        kt = jnp.moveaxis(k, 1, 0)
        vt = jnp.moveaxis(v, 1, 0)
        at = jnp.moveaxis(alpha, 1, 0)
        bt = jnp.moveaxis(beta, 1, 0)
        state0 = jnp.zeros((batch, H, hd, hd), dtype=x.dtype)

        def step(state, inp):
            q_t, k_t, v_t, a_t, b_t = inp
            pred = jnp.einsum('bhde,bhd->bhe', state, k_t)
            error = v_t - pred
            update = jnp.einsum('bhe,bhd->bhde', b_t[..., None] * error, k_t)
            state = a_t[..., None, None] * state + update
            out = jnp.einsum('bhde,bhd->bhe', state, q_t)
            return (state, out)
        _, ys = lax.scan(step, state0, (qt, kt, vt, at, bt))
        y = jnp.moveaxis(ys, 0, 1).reshape(batch, seq_len, d_model)
        gate = jax.nn.silu(residual_input @ Wg)
        y = _rmsnorm(y, g_norm) * gate
        return y @ Wo

    def _L0_ffn_ref(x, expert_weights, expert_indices, w1_A, w1_B, w2_A, w2_B):
        import jax, jax.numpy as jnp
        import numpy as np
        SL, BS, HS = (512, 4, 256)
        FF = 1024
        E, RANK, TOPK = (8, 64, 2)
        sl, bs, hs = x.shape
        T = sl * bs
        top_k = expert_indices.shape[-1]
        flat_e = expert_indices.reshape(-1)
        flat_w = expert_weights.reshape(-1)
        order = jnp.argsort(flat_e, stable=True)
        bin_ids = flat_e[order]
        tok = order // top_k
        xr = x.reshape(T, hs)[tok]
        w1A = w1_A.reshape(E, RANK, hs)
        w1B = w1_B.reshape(E, RANK, FF)
        w2A = w2_A.reshape(E, RANK, FF)
        w2B = w2_B.reshape(E, RANK, hs)
        out = jnp.zeros_like(xr)
        for e in range(E):
            mask = (bin_ids == e).astype(xr.dtype)[:, None]
            h = jax.nn.gelu(xr @ w1A[e].T @ w1B[e], approximate=False)
            ye = h @ w2A[e].T @ w2B[e]
            out = out + mask * ye
        y = jnp.zeros((T, hs), xr.dtype).at[tok].add(flat_w[order][:, None] * out)
        return y.reshape(sl, bs, hs)
    x = L0_attn_x
    x = x + 0.5 * _L0_ffn_ref(_layernorm(x, axis=-1), L0_ffn_expert_weights, L0_ffn_expert_indices, L0_ffn_w1_A, L0_ffn_w1_B, L0_ffn_w2_A, L0_ffn_w2_B)
    x = x + _L0_attn_ref(_layernorm(x, axis=-1), L0_attn_Wq, L0_attn_Wk, L0_attn_Wv, L0_attn_Wa, L0_attn_ba, L0_attn_Wb, L0_attn_bb, L0_attn_Wg, L0_attn_Wo, L0_attn_g_norm)
    x = x + 0.5 * _L0_ffn_ref(_layernorm(x, axis=-1), L0_ffn_expert_weights, L0_ffn_expert_indices, L0_ffn_w1_A, L0_ffn_w1_B, L0_ffn_w2_A, L0_ffn_w2_B)
    return x

_drawn_inputs = setup_inputs


def setup_inputs(seed=0):
    import zlib

    import numpy as np

    out = dict(_drawn_inputs(seed))
    spreads = {'L0_attn_ba': (0.0, 2.0), 'L0_attn_bb': (0.0, 2.0), 'L0_attn_g_norm': (1.0, 0.6)}
    factors = {'L0_ffn_expert_weights': 8.0,
     'L0_ffn_w1_A': 8.0,
     'L0_ffn_w1_B': 8.0,
     'L0_ffn_w2_A': 8.0,
     'L0_ffn_w2_B': 8.0,
     'L0_attn_Wq': 3.439,
     'L0_attn_Wk': 3.429,
     'L0_attn_Wv': 3.393,
     'L0_attn_Wa': 8.0,
     'L0_attn_Wb': 8.0,
     'L0_attn_Wg': 3.632,
     'L0_attn_Wo': 3.428}
    for name, (base, spread) in spreads.items():
        noise = np.random.default_rng([zlib.crc32(name.encode()), seed]).standard_normal(out[name].shape)
        drawn = base * np.exp(spread * noise) if base else spread * noise
        out[name] = jnp.asarray(drawn.astype(out[name].dtype))
    for name, factor in factors.items():
        out[name] = (out[name] * factor).astype(out[name].dtype)
    return out
```

```python
from contextlib import ExitStack

import concourse.bass as bass
import numpy as np
from concourse import mybir

F32 = mybir.dt.float32
F32R = mybir.dt.float32r
I32 = mybir.dt.int32
ALU = mybir.AluOpType
ACT = mybir.ActivationFunctionType
AX = mybir.AxisListType

P = 128
D = 256
KT = D // P
EPS = 1e-5

T_FFN = 2048
BATCHES = 8
SEQ = 1024
FFN_BATCHES = T_FFN // SEQ
TOPK = 2
E = 8
RANK = 64
FF = 1024
FT = FF // P
TT = T_FFN // P
PAIRS = TT * TOPK
SLOT_TILES = 40
SLOTS = SLOT_TILES * P
PEELED = 4
DUMP = T_FFN * TOPK


class Step:

    def __init__(self, i, off):
        self.i, self.off = i, off
        self.p = off % 2
        self.j = i * 2 + off
        self.half = i + off // 2

    def plus(self, n):
        return Step(self.i, self.off + n)


class Stage(ExitStack):

    def __init__(self, nc):
        super().__init__()
        self.nc, self.held = nc, []

    def semaphore(self, name):
        self.held.append(self.nc.alloc_semaphore(name))
        return self.held[-1]

    def __exit__(self, *exc):
        done = super().__exit__(*exc)
        if self.held and exc[0] is None:
            self.nc.clear_and_free_semaphores(self.held)
            self.nc.all_engine_barrier()
        return done


def at_least(eng, sem, n):
    if isinstance(n, int):
        if n > 0:
            eng.wait_ge(sem, n)
        return
    assert n.min_val > 0
    eng.wait_ge(sem, n)


def run_steps(eng, body, n, first=2, last=2):
    for j in range(first):
        body(Step(0, j))
    if n - first - last > 0:
        with eng.Fori(0, (n - first - last) // 2) as i:
            for u in range(2):
                body(Step(i, first + u))
    for j in range(n - last, n):
        body(Step(0, j))


def routing(nc, expert_indices, expert_weights, c, rt):
    with Stage(nc) as ctx:
        idx_i = ctx.enter_context(nc.sbuf_tensor("idx_i", [P, PAIRS], I32))
        idx_f = ctx.enter_context(nc.sbuf_tensor("idx_f", [P, PAIRS], F32))
        wts = ctx.enter_context(nc.sbuf_tensor("wts", [P, PAIRS], F32))
        onehot = ctx.enter_context(nc.sbuf_tensor("onehot", [P, PAIRS, E], F32))
        upto = ctx.enter_context(nc.sbuf_tensor("upto", [P, PAIRS, E], F32))
        place = ctx.enter_context(nc.sbuf_tensor("place", [P, PAIRS, E], F32))
        ones_pe = ctx.enter_context(nc.sbuf_tensor("ones_pe", [P, PAIRS], F32))
        cmp = ctx.enter_context(nc.sbuf_tensor("cmp", [P, E, PAIRS], F32))
        cmp2 = ctx.enter_context(nc.sbuf_tensor("cmp2", [1, SLOT_TILES, E], F32))
        ntile = ctx.enter_context(nc.sbuf_tensor("ntile", [P, E], F32))
        endt = ctx.enter_context(nc.sbuf_tensor("endt", [P, E], F32))
        base = ctx.enter_context(nc.sbuf_tensor("base", [P, E], F32))
        texp_f = ctx.enter_context(nc.sbuf_tensor("texp_f", [1, SLOT_TILES], F32))
        pos_f = ctx.enter_context(nc.sbuf_tensor("pos_f", [P, PAIRS], F32))
        valid = ctx.enter_context(nc.sbuf_tensor("valid", [P, PAIRS], F32))
        zero_rows = ctx.enter_context(nc.sbuf_tensor("zero_rows", [P, 10 * D], F32))
        ps_within = ctx.enter_context(nc.psum_tensor("ps_within", [P, PAIRS * E], F32))
        ps_total = ctx.enter_context(nc.psum_tensor("ps_total", [P, PAIRS * E], F32))
        loaded = ctx.semaphore("r_loaded")
        onehot_ready = ctx.semaphore("r_onehot")
        counts_ready = ctx.semaphore("r_counts")
        chain = ctx.semaphore("r_chain")
        zero_ready = ctx.semaphore("r_zero")
        cleared = ctx.semaphore("r_cleared")
        block = ctx.enter_context(nc.Block())

        @block.sync
        def _(sp):
            sp.dma_start(idx_i[:].rearrange("p (i k) -> p i k", k=TOPK),
                         expert_indices.rearrange("(i p) k -> p i k", p=P)).then_inc(loaded, 16)
            sp.dma_start(wts[:].rearrange("p (i k) -> p i k", k=TOPK),
                         expert_weights.rearrange("(i p) k -> p i k", p=P)).then_inc(loaded, 16)
            sp.wait_ge(zero_ready, 1)
            for n in range(SLOT_TILES // 10):
                sp.dma_start(rt["xs"][n * 10 * P:(n + 1) * 10 * P, :].rearrange("(p r) d -> p (r d)", r=10),
                             zero_rows[:]).then_inc(cleared, 16)
            sp.wait_ge(cleared, 16 * (SLOT_TILES // 10))

        @block.gpsimd
        def _(pool):
            pool.memset(zero_rows[:], 0.0).then_inc(zero_ready, 1)

        @block.tensor
        def _(pe):
            pe.wait_ge(onehot_ready, 1)
            pe.matmul(ps_within[:], c["before"][:], onehot[:].rearrange("p a e -> p (a e)"), start=True, stop=True)
            pe.matmul(ps_total[:], c["ones"][:], onehot[:].rearrange("p a e -> p (a e)"),
                      start=True, stop=True).then_inc(counts_ready, 1)

        @block.vector
        def _(dve):
            n = [0]

            def then(ins):
                n[0] += 1
                ins.then_inc(chain, 1)
                dve.wait_ge(chain, n[0])

            dve.wait_ge(loaded, 32)
            then(dve.tensor_copy(idx_f[:], idx_i[:]))
            dve.memset(ones_pe[:], 1.0)
            dve.tensor_tensor(onehot[:], idx_f[:].unsqueeze(2).broadcast_to([P, PAIRS, E]),
                              c["iota_e"][:].unsqueeze(1).broadcast_to([P, PAIRS, E]),
                              ALU.is_equal).then_inc(onehot_ready, 1)
            dve.wait_ge(counts_ready, 1)
            tot = ps_total[:].rearrange("p (a e) -> p a e", e=E)
            within = ps_within[:].rearrange("p (a e) -> p a e", e=E)
            for e in range(E):
                last = dve.tensor_tensor_scan(upto[:, :, e], ones_pe[:], tot[:, :, e], 0.0, ALU.mult, ALU.add)
            then(last)
            then(dve.tensor_tensor(cmp[:], upto[:, PAIRS - 1, :].unsqueeze(2).broadcast_to([P, E, PAIRS]),
                                   c["iota_128"][:].unsqueeze(1).broadcast_to([P, E, PAIRS]), ALU.is_gt))
            then(dve.tensor_reduce(ntile[:], cmp[:], AX.X, ALU.add))
            then(dve.tensor_tensor_scan(endt[:], ones_pe[:, 0:E], ntile[:], 0.0, ALU.mult, ALU.add))
            then(dve.tensor_tensor(base[:], endt[:], ntile[:], ALU.subtract))
            then(dve.tensor_scalar(base[:], base[:], float(P), None, ALU.mult))
            then(dve.tensor_tensor(upto[:], upto[:], tot, ALU.subtract))
            then(dve.tensor_tensor(place[:], upto[:], within, ALU.add))
            then(dve.tensor_tensor(place[:], place[:], base[:].unsqueeze(1).broadcast_to([P, PAIRS, E]), ALU.add))
            then(dve.tensor_tensor(place[:], place[:], onehot[:], ALU.mult))
            then(dve.tensor_reduce(pos_f[:], place[:], AX.X, ALU.add))
            then(dve.tensor_reduce(valid[:], onehot[:], AX.X, ALU.add))
            then(dve.tensor_copy(rt["pos_gather"][:], pos_f[:]))
            then(dve.tensor_tensor(wts[:], wts[:], valid[:], ALU.mult))
            then(dve.tensor_scalar(rt["half_w"][:], wts[:], 0.5, None, ALU.mult))
            then(dve.tensor_scalar(valid[:], valid[:], -1.0, 1.0, ALU.mult, ALU.add))
            then(dve.tensor_tensor(valid[:], valid[:], c["dump_row"][:], ALU.mult))
            then(dve.tensor_tensor(pos_f[:], pos_f[:], valid[:], ALU.add))
            then(dve.tensor_copy(rt["pos_scatter"][:], pos_f[:]))
            then(dve.tensor_tensor(cmp2[:], endt[0:1, :].unsqueeze(1).broadcast_to([1, SLOT_TILES, E]),
                                   c["iota_tile"][:].unsqueeze(2).broadcast_to([1, SLOT_TILES, E]), ALU.is_le))
            then(dve.tensor_reduce(texp_f[:], cmp2[:], AX.X, ALU.add))
            then(dve.tensor_scalar(texp_f[:], texp_f[:], float(E - 1), None, ALU.min))
            then(dve.tensor_copy(rt["tile_expert"][:], texp_f[:]))


def ffn_rows(a):
    return a.rearrange("(i r b) d -> i r b d", r=P // FFN_BATCHES, b=BATCHES)[:, :, 0:FFN_BATCHES]


def ffn_scatter(nc, name, src, c, rt):
    with Stage(nc) as ctx:
        xt = ctx.enter_context(nc.sbuf_tensor(f"{name}_x", [P, 4, D], F32))
        xn = ctx.enter_context(nc.sbuf_tensor(f"{name}_xn", [P, 4, D], F32))
        st = ctx.enter_context(nc.sbuf_tensor(f"{name}_st", [P, 4, 6], F32))
        mv = ctx.enter_context(nc.sbuf_tensor(f"{name}_mv", [P, 4, 2], F32))
        sd = ctx.enter_context(nc.sbuf_tensor(f"{name}_sd", [P, 4], F32))
        rs = ctx.enter_context(nc.sbuf_tensor(f"{name}_rs", [P, 4], F32))
        in0 = ctx.semaphore(f"{name}_in0")
        in1 = ctx.semaphore(f"{name}_in1")
        in2 = ctx.semaphore(f"{name}_in2")
        in3 = ctx.semaphore(f"{name}_in3")
        var_ready = ctx.semaphore(f"{name}_var")
        std_ready = ctx.semaphore(f"{name}_std")
        norm_ready = ctx.semaphore(f"{name}_norm")
        chain = ctx.semaphore(f"{name}_chain")
        out0 = ctx.semaphore(f"{name}_out0")
        out1 = ctx.semaphore(f"{name}_out1")
        out2 = ctx.semaphore(f"{name}_out2")
        out3 = ctx.semaphore(f"{name}_out3")
        block = ctx.enter_context(nc.Block())
        row_in, row_out = [in0, in1, in2, in3], [out0, out1, out2, out3]
        src_t = ffn_rows(src)

        @block.sync
        def _(sp):
            for i in range(TT):
                if i >= 4:
                    sp.wait_ge(norm_ready, i - 3)
                sp.dma_start(xt[:, i % 4], src_t[i]).then_inc(row_in[i % 4], 16)

        @block.scalar
        def _(act):
            for i in range(TT):
                act.wait_ge(var_ready, i + 1)
                act.activation(sd[:, i % 4:i % 4 + 1], mv[:, i % 4, 1:2], ACT.Sqrt,
                               bias=c["eps"][:, 0:1]).then_inc(std_ready, 1)

        @block.vector
        def _(dve):
            n = [0]

            def then(ins):
                n[0] += 1
                ins.then_inc(chain, 1)
                dve.wait_ge(chain, n[0])

            def moments(i):
                dve.wait_ge(row_in[i % 4], 16 * (i // 4 + 1))
                if i >= 4:
                    dve.wait_ge(var_ready, i - 3)
                then(dve.bn_stats(st[:, i % 4], xt[:, i % 4]))
                dve.bn_aggr(mv[:, i % 4], st[:, i % 4]).then_inc(var_ready, 1)

            def normalise(i):
                dve.wait_ge(std_ready, i + 1)
                then(dve.reciprocal(rs[:, i % 4:i % 4 + 1], sd[:, i % 4:i % 4 + 1]))
                if i >= 4:
                    dve.wait_ge(row_out[i % 4], 32 * (i // 4))
                dve.tensor_scalar(xn[:, i % 4], xt[:, i % 4], mv[:, i % 4, 0:1], rs[:, i % 4:i % 4 + 1],
                                  ALU.subtract, ALU.mult).then_inc(norm_ready, 1)

            moments(0)
            for i in range(TT):
                if i + 1 < TT:
                    if i >= 3:
                        dve.wait_ge(norm_ready, i - 2)
                    moments(i + 1)
                normalise(i)

        @block.gpsimd
        def _(pool):
            for i in range(TT):
                pool.wait_ge(norm_ready, i + 1)
                for k in range(TOPK):
                    col = i * TOPK + k
                    pool.indirect_dma_start(
                        rt["xs"], bass.IndirectOffsetOnAxis(ap=rt["pos_scatter"][:, col:col + 1], axis=0),
                        xn[:, i % 4], None).then_inc(row_out[i % 4], 16)
            for m in range(4):
                pool.wait_ge(row_out[m], 32 * (TT // 4))


def ffn_experts(nc, name, w, c, rt):
    w1a_t, w1b, w2a_t, w2b = w
    n_stage = 4
    with Stage(nc) as ctx:
        w1a_hl = ctx.enter_context(nc.sbuf_tensor(f"{name}_w1a", [P, KT, E, 2 * RANK], F32R))
        w1b_h = ctx.enter_context(nc.sbuf_tensor(f"{name}_w1bh", [P, E, FF], F32R))
        w1b_l = ctx.enter_context(nc.sbuf_tensor(f"{name}_w1bl", [P, E, FF], F32R))
        w2a_hl = ctx.enter_context(nc.sbuf_tensor(f"{name}_w2a", [P, FT, E, 2 * RANK], F32R))
        w2b_h = ctx.enter_context(nc.sbuf_tensor(f"{name}_w2bh", [P, E, D], F32R))
        w2b_l = ctx.enter_context(nc.sbuf_tensor(f"{name}_w2bl", [P, E, D], F32R))
        raw = ctx.enter_context(nc.sbuf_tensor(f"{name}_raw", [P, n_stage, FF], F32))
        xs = ctx.enter_context(nc.sbuf_tensor(f"{name}_xs", [P, 2, D], F32))
        xh = ctx.enter_context(nc.sbuf_tensor(f"{name}_xh", [P, KT, P], F32R))
        xl = ctx.enter_context(nc.sbuf_tensor(f"{name}_xl", [P, KT, P], F32R))
        part = ctx.enter_context(nc.sbuf_tensor(f"{name}_part", [P, 2, RANK], F32))
        h1 = ctx.enter_context(nc.sbuf_tensor(f"{name}_h1", [P, 2, RANK], F32))
        h1_stack = ctx.enter_context(nc.sbuf_tensor(f"{name}_h1s", [P, 2, P], F32R))
        hg = ctx.enter_context(nc.sbuf_tensor(f"{name}_hg", [P, FF], F32))
        hh = ctx.enter_context(nc.sbuf_tensor(f"{name}_hh", [P, FT, P], F32R))
        hl = ctx.enter_context(nc.sbuf_tensor(f"{name}_hl", [P, FT, P], F32R))
        y1 = ctx.enter_context(nc.sbuf_tensor(f"{name}_y1", [P, 2, RANK], F32))
        y1_stack = ctx.enter_context(nc.sbuf_tensor(f"{name}_y1s", [P, P], F32R))
        ys = ctx.enter_context(nc.sbuf_tensor(f"{name}_ys", [P, 2, D], F32))
        ps_x = ctx.enter_context(nc.psum_tensor(f"{name}_psx", [P, KT, P], F32))
        ps_a = ctx.enter_context(nc.psum_tensor(f"{name}_psa", [P, 512], F32))
        ps_b = ctx.enter_context(nc.psum_tensor(f"{name}_psb", [P, 2, 512], F32))
        ps_h = ctx.enter_context(nc.psum_tensor(f"{name}_psh", [P, FT, P], F32))
        ps_c = ctx.enter_context(nc.psum_tensor(f"{name}_psc", [P, 512], F32))
        ps_d = ctx.enter_context(nc.psum_tensor(f"{name}_psd", [P, 512], F32))
        ps_h1t = ps_a[:, 2 * RANK:2 * RANK + P]
        ps_y1t = ps_c[:, 2 * RANK:2 * RANK + P]

        jobs = []
        for k in range(KT):
            v = w1a_t[k * P:(k + 1) * P, :]
            jobs.append((v, E * RANK, None, w1a_hl[:, k, :, 0:RANK], w1a_hl[:, k, :, RANK:2 * RANK], RANK))
        for f in range(FT):
            v = w2a_t[f * P:(f + 1) * P, :]
            jobs.append((v, E * RANK, None, w2a_hl[:, f, :, 0:RANK], w2a_hl[:, f, :, RANK:2 * RANK], RANK))
        for e in range(E):
            jobs.append((w1b[e * RANK:(e + 1) * RANK, :], FF, "twice", w1b_h[:, e], w1b_l[:, e], None))
        for e in range(0, E, 4):
            v = w2b[e * RANK:(e + 4) * RANK, :].rearrange("(e r) d -> r e d", r=RANK)
            jobs.append((v, 4 * D, "twice4", w2b_h[:, e:e + 4], w2b_l[:, e:e + 4], D))
        with Stage(nc) as ctx:
            raw0 = ctx.semaphore(f"{name}_raw0")
            raw1 = ctx.semaphore(f"{name}_raw1")
            raw2 = ctx.semaphore(f"{name}_raw2")
            raw3 = ctx.semaphore(f"{name}_raw3")
            high_ready = ctx.semaphore(f"{name}_high")
            low_ready = ctx.semaphore(f"{name}_low")
            block = ctx.enter_context(nc.Block())
            raw_in = [raw0, raw1, raw2, raw3]
            need = [[] for _ in jobs]
            so_far = [0] * n_stage
            for n, job in enumerate(jobs):
                so_far[n % n_stage] += 32 if job[2] else 16
                need[n] = so_far[n % n_stage]

            def shaped(ap, width):
                return ap if width is None else ap.rearrange("p (e r) -> p e r", r=width)

            @block.sync
            def _(sp):
                for n, (v, size, kind, _h, _l, width) in enumerate(jobs):
                    if n >= n_stage:
                        sp.wait_ge(low_ready, n - n_stage + 1)
                    if kind is None:
                        sp.dma_start(raw[:, n % n_stage, 0:size], v).then_inc(raw_in[n % n_stage], 16)
                    else:
                        for r in range(2):
                            dst = raw[r * RANK:(r + 1) * RANK, n % n_stage, 0:size]
                            if kind == "twice4":
                                dst = dst.rearrange("p (e d) -> p e d", d=D)
                            sp.dma_start(dst, v).then_inc(raw_in[n % n_stage], 16)

            @block.scalar
            def _(act):
                for n, (_v, size, _k, high, _l, width) in enumerate(jobs):
                    act.wait_ge(raw_in[n % n_stage], need[n])
                    act.activation(high, shaped(raw[:, n % n_stage, 0:size], width), ACT.Copy).then_inc(high_ready, 1)

            @block.vector
            def _(dve):
                for n, (_v, size, _k, high, low, width) in enumerate(jobs):
                    dve.wait_ge(high_ready, n + 1)
                    dve.wait_ge(raw_in[n % n_stage], need[n])
                    dve.tensor_tensor(low, shaped(raw[:, n % n_stage, 0:size], width), high.bitcast(F32),
                                      ALU.subtract).then_inc(low_ready, 1)

        names = ["xs0", "xs1", "xt", "xh", "xl", "a", "ap", "h1", "h1t", "h1h", "h1s", "b", "g0", "g1", "ht0", "ht1",
                 "hh0", "hh1", "hl0", "hl1", "c", "cp", "y1", "y1t", "y1h", "y1s", "d", "ys", "st0", "st1"]
        with Stage(nc) as ctx:
            s = {n: ctx.semaphore(f"{name}_s_" + n) for n in names}
            block = ctx.enter_context(nc.Block())
            xs_tiles = rt["xs"][0:SLOTS, :].rearrange("(t p) d -> p t d", p=P)
            ys_tiles = rt["ys"].rearrange("(t p) d -> p t d", p=P)

            @block.sync
            def _(sp):
                def load(t):
                    at_least(sp, s["xt"], t.j - 1)
                    sp.dma_start(xs[:, t.p:t.p + 1], xs_tiles[:, bass.ds(t.j, 1), :]).then_inc(s[f"xs{t.p}"], 16)

                run_steps(sp, load, SLOT_TILES)

            @block.tensor
            def _(pe):
                ident = c["ident"][:]

                def transpose_x(t):
                    pe.wait_ge(s[f"xs{t.p}"], (t.half + 1) * 16)
                    at_least(pe, s["xl"], t.j)
                    for k in range(KT):
                        last = pe.transpose(ps_x[:, k], xs[:, t.p, k * P:(k + 1) * P], ident)
                    last.then_inc(s["xt"], 1)

                def first_down(t, e):
                    pe.wait_ge(s["xh"], t.j + 1)
                    pe.wait_ge(s["xl"], t.j + 1)
                    at_least(pe, s["h1s"], t.j)
                    at_least(pe, s["h1"], t.j)
                    for k in range(KT):
                        pe.matmul(ps_a[:, 0:2 * RANK], xh[:, k], w1a_hl[:, k, bass.ds(e, 1), :].rearrange("p a r -> p (a r)"),
                                  start=(k == 0), stop=False, skip_group_check=True)
                    for k in range(KT):
                        last = pe.matmul(ps_a[:, 0:RANK], xl[:, k],
                                         w1a_hl[:, k, bass.ds(e, 1), 0:RANK].rearrange("p a r -> p (a r)"),
                                         start=False, stop=(k == KT - 1), skip_group_check=True)
                    last.then_inc(s["a"], 1)

                def transpose_h1(t):
                    pe.wait_ge(s["h1"], t.j + 1)
                    pe.transpose(ps_h1t, h1[:].rearrange("p a r -> p (a r)"), ident).then_inc(s["h1t"], 1)

                def first_up(t, e):
                    pe.wait_ge(s["h1s"], t.j + 1)
                    for n in range(2):
                        at_least(pe, s[f"g{n}"], t.j)
                        for m, wt in enumerate((w1b_h, w1b_l)):
                            last = pe.matmul(ps_b[:, n], h1_stack[:, t.p],
                                             wt[:, bass.ds(e, 1), n * 512:(n + 1) * 512].rearrange("p a f -> p (a f)"),
                                             start=(m == 0), stop=(m == 1))
                        last.then_inc(s["b"], 1)

                def transpose_h(t, n):
                    pe.wait_ge(s[f"g{n}"], t.j + 1)
                    at_least(pe, s[f"hl{n}"], t.j)
                    for f in range(4 * n, 4 * n + 4):
                        last = pe.transpose(ps_h[:, f], hg[:, f * P:(f + 1) * P], ident)
                    last.then_inc(s[f"ht{n}"], 1)

                def second_down(t, e):
                    at_least(pe, s["y1"], t.j)
                    at_least(pe, s["y1s"], t.j)
                    for n in range(2):
                        pe.wait_ge(s[f"hh{n}"], t.j + 1)
                        pe.wait_ge(s[f"hl{n}"], t.j + 1)
                        for f in range(4 * n, 4 * n + 4):
                            pe.matmul(ps_c[:, 0:2 * RANK], hh[:, f], w2a_hl[:, f, bass.ds(e, 1), :].rearrange("p a r -> p (a r)"),
                                      start=(f == 0), stop=False, skip_group_check=True)
                            last = pe.matmul(ps_c[:, 0:RANK], hl[:, f],
                                             w2a_hl[:, f, bass.ds(e, 1), 0:RANK].rearrange("p a r -> p (a r)"),
                                             start=False, stop=(f == FT - 1), skip_group_check=True)
                    last.then_inc(s["c"], 1)

                def transpose_y1(t):
                    pe.wait_ge(s["y1"], t.j + 1)
                    pe.transpose(ps_y1t, y1[:].rearrange("p a r -> p (a r)"), ident).then_inc(s["y1t"], 1)

                def second_up(t, e):
                    pe.wait_ge(s["y1s"], t.j + 1)
                    at_least(pe, s["ys"], t.j)
                    for m, wt in enumerate((w2b_h, w2b_l)):
                        last = pe.matmul(ps_d[:, 0:D], y1_stack[:], wt[:, bass.ds(e, 1), :].rearrange("p a d -> p (a d)"),
                                         start=(m == 0), stop=(m == 1))
                    last.then_inc(s["d"], 1)

                def expert(t):
                    return pe.value_load(rt["tile_expert"][0:1, bass.ds(t.j, 1)], min_val=0, max_val=E - 1)

                def step(t, first=False, final=False):
                    e = expert(t)
                    first_up(t, e)
                    if not final:
                        transpose_x(t.plus(1))
                    if not first:
                        transpose_y1(t.plus(-1))
                    transpose_h(t, 0)
                    if not final:
                        first_down(t.plus(1), expert(t.plus(1)))
                    transpose_h(t, 1)
                    if not first:
                        second_up(t.plus(-1), expert(t.plus(-1)))
                    if not final:
                        transpose_h1(t.plus(1))
                    second_down(t, e)

                t0 = Step(0, 0)
                transpose_x(t0)
                first_down(t0, expert(t0))
                transpose_h1(t0)
                step(t0, first=True)
                for j in range(1, PEELED):
                    step(Step(0, j))
                with pe.Fori(0, (SLOT_TILES - PEELED - 2) // 2) as i:
                    for u in range(2):
                        step(Step(i, PEELED + u))
                step(Step(0, SLOT_TILES - 2))
                t_end = Step(0, SLOT_TILES - 1)
                step(t_end, final=True)
                transpose_y1(t_end)
                second_up(t_end, expert(t_end))

            @block.scalar
            def _(act):
                def x_high(t):
                    act.wait_ge(s["xt"], t.j + 1)
                    at_least(act, s["a"], t.j)
                    act.activation(xh[:], ps_x[:], ACT.Copy).then_inc(s["xh"], 1)

                def h1_part(t):
                    act.wait_ge(s["a"], t.j + 1)
                    at_least(act, s["h1"], t.j)
                    act.activation(part[:, 0], ps_a[:, RANK:2 * RANK], ACT.Copy).then_inc(s["ap"], 1)

                def h1_high(t):
                    act.wait_ge(s["h1t"], t.j + 1)
                    at_least(act, s["b"], (t.j - 1) * 2)
                    act.activation(h1_stack[:, t.p], ps_h1t, ACT.Copy).then_inc(s["h1h"], 1)

                def gelu(t, n):
                    act.wait_ge(s["b"], t.j * 2 + n + 1)
                    at_least(act, s[f"ht{n}"], t.j)
                    act.activation(hg[:, n * 512:(n + 1) * 512], ps_b[:, n], ACT.Gelu).then_inc(s[f"g{n}"], 1)

                def h_high(t, n):
                    act.wait_ge(s[f"ht{n}"], t.j + 1)
                    at_least(act, s["c"], t.j)
                    act.activation(hh[:, 4 * n:4 * n + 4], ps_h[:, 4 * n:4 * n + 4], ACT.Copy).then_inc(s[f"hh{n}"], 1)

                def y1_part(t):
                    act.wait_ge(s["c"], t.j + 1)
                    at_least(act, s["y1"], t.j)
                    act.activation(part[:, 1], ps_c[:, RANK:2 * RANK], ACT.Copy).then_inc(s["cp"], 1)

                def y1_high(t):
                    act.wait_ge(s["y1t"], t.j + 1)
                    at_least(act, s["d"], t.j)
                    act.activation(y1_stack[:], ps_y1t, ACT.Copy).then_inc(s["y1h"], 1)

                def y_out(t):
                    act.wait_ge(s["d"], t.j + 1)
                    at_least(act, s[f"st{t.p}"], t.half * 16)
                    act.activation(ys[:, t.p], ps_d[:, 0:D], ACT.Copy).then_inc(s["ys"], 1)
                    act.wait_ge(s["ys"], t.j + 1)
                    act.dma_start(ys_tiles[:, bass.ds(t.j, 1), :], ys[:, t.p:t.p + 1]).then_inc(s[f"st{t.p}"], 16)

                def step(t, first=False, final=False):
                    gelu(t, 0)
                    if not final:
                        x_high(t.plus(1))
                    if not first:
                        y1_high(t.plus(-1))
                    gelu(t, 1)
                    h_high(t, 0)
                    if not final:
                        h1_part(t.plus(1))
                    h_high(t, 1)
                    if not first:
                        y_out(t.plus(-1))
                    if not final:
                        h1_high(t.plus(1))
                    y1_part(t)

                t0 = Step(0, 0)
                x_high(t0)
                h1_part(t0)
                h1_high(t0)
                step(t0, first=True)
                for j in range(1, PEELED):
                    step(Step(0, j))
                with act.Fori(0, (SLOT_TILES - PEELED - 2) // 2) as i:
                    for u in range(2):
                        step(Step(i, PEELED + u))
                step(Step(0, SLOT_TILES - 2))
                t_end = Step(0, SLOT_TILES - 1)
                step(t_end, final=True)
                y1_high(t_end)
                y_out(t_end)
                for p in range(2):
                    act.wait_ge(s[f"st{p}"], 16 * (SLOT_TILES // 2))

            @block.vector
            def _(dve):
                def x_low(t):
                    dve.wait_ge(s["xh"], t.j + 1)
                    at_least(dve, s["a"], t.j)
                    dve.tensor_tensor(xl[:], ps_x[:], xh[:].bitcast(F32), ALU.subtract).then_inc(s["xl"], 1)

                def h1_sum(t):
                    dve.wait_ge(s["ap"], t.j + 1)
                    at_least(dve, s["h1t"], t.j)
                    dve.tensor_tensor(h1[:], ps_a[:, 0:RANK].unsqueeze(1).broadcast_to([P, 2, RANK]),
                                      part[:, 0].unsqueeze(1).broadcast_to([P, 2, RANK]), ALU.add).then_inc(s["h1"], 1)

                def h1_low(t):
                    dve.wait_ge(s["h1h"], t.j + 1)
                    low = h1_stack[RANK:P, t.p]
                    dve.tensor_tensor(low, ps_h1t[RANK:P], low.bitcast(F32), ALU.subtract).then_inc(s["h1s"], 1)

                def h_low(t, n):
                    dve.wait_ge(s[f"hh{n}"], t.j + 1)
                    at_least(dve, s["c"], t.j)
                    dve.tensor_tensor(hl[:, 4 * n:4 * n + 4], ps_h[:, 4 * n:4 * n + 4],
                                      hh[:, 4 * n:4 * n + 4].bitcast(F32), ALU.subtract).then_inc(s[f"hl{n}"], 1)

                def y1_sum(t):
                    dve.wait_ge(s["cp"], t.j + 1)
                    at_least(dve, s["y1t"], t.j)
                    dve.tensor_tensor(y1[:], ps_c[:, 0:RANK].unsqueeze(1).broadcast_to([P, 2, RANK]),
                                      part[:, 1].unsqueeze(1).broadcast_to([P, 2, RANK]), ALU.add).then_inc(s["y1"], 1)

                def y1_low(t):
                    dve.wait_ge(s["y1h"], t.j + 1)
                    low = y1_stack[RANK:P, :]
                    dve.tensor_tensor(low, ps_y1t[RANK:P], low.bitcast(F32), ALU.subtract).then_inc(s["y1s"], 1)

                def step(t, first=False, final=False):
                    if not final:
                        x_low(t.plus(1))
                    if not first:
                        y1_low(t.plus(-1))
                    h_low(t, 0)
                    if not final:
                        h1_sum(t.plus(1))
                    h_low(t, 1)
                    if not final:
                        h1_low(t.plus(1))
                    y1_sum(t)

                t0 = Step(0, 0)
                x_low(t0)
                h1_sum(t0)
                h1_low(t0)
                step(t0, first=True)
                for j in range(1, PEELED):
                    step(Step(0, j))
                with dve.Fori(0, (SLOT_TILES - PEELED - 2) // 2) as i:
                    for u in range(2):
                        step(Step(i, PEELED + u))
                step(Step(0, SLOT_TILES - 2))
                t_end = Step(0, SLOT_TILES - 1)
                step(t_end, final=True)
                y1_low(t_end)


def ffn_combine(nc, name, src, dst, c, rt):
    nb = 4
    with Stage(nc) as ctx:
        xt = ctx.enter_context(nc.sbuf_tensor(f"{name}_x", [P, nb, D], F32))
        y = ctx.enter_context(nc.sbuf_tensor(f"{name}_y", [P, nb, TOPK, D], F32))
        x_in = [ctx.semaphore(f"{name}_xin{m}") for m in range(nb)]
        y_in = [ctx.semaphore(f"{name}_yin{m}") for m in range(nb)]
        added = ctx.semaphore(f"{name}_added")
        summed = ctx.semaphore(f"{name}_summed")
        stored = [ctx.semaphore(f"{name}_stored{m}") for m in range(nb)]
        block = ctx.enter_context(nc.Block())
        src_t, dst_t = ffn_rows(src), ffn_rows(dst)

        @block.sync
        def _(sp):
            for i in range(TT):
                if i >= nb:
                    sp.wait_ge(stored[i % nb], 16 * (i // nb))
                sp.dma_start(xt[:, i % nb], src_t[i]).then_inc(x_in[i % nb], 16)

        @block.gpsimd
        def _(pool):
            for i in range(TT):
                if i >= nb:
                    pool.wait_ge(summed, i - nb + 1)
                for k in range(TOPK):
                    col = i * TOPK + k
                    pool.indirect_dma_start(
                        y[:, i % nb, k], None, rt["ys"],
                        bass.IndirectOffsetOnAxis(ap=rt["pos_gather"][:, col:col + 1], axis=0)).then_inc(y_in[i % nb], 16)

        @block.vector
        def _(dve):
            for i in range(TT):
                m = i % nb
                dve.wait_ge(x_in[m], 16 * (i // nb + 1))
                dve.wait_ge(y_in[m], 32 * (i // nb + 1))
                dve.scalar_tensor_tensor(xt[:, m], y[:, m, 0], rt["half_w"][:, i * TOPK:i * TOPK + 1], xt[:, m],
                                         ALU.mult, ALU.add).then_inc(added, 1)
                dve.wait_ge(added, i + 1)
                dve.scalar_tensor_tensor(xt[:, m], y[:, m, 1], rt["half_w"][:, i * TOPK + 1:i * TOPK + 2], xt[:, m],
                                         ALU.mult, ALU.add).then_inc(summed, 1)

        @block.scalar
        def _(act):
            for i in range(TT):
                act.wait_ge(summed, i + 1)
                act.dma_start(dst_t[i], xt[:, i % nb]).then_inc(stored[i % nb], 16)
            for m in range(nb):
                act.wait_ge(stored[m], 16 * (TT // nb))


H = 16
HD = D // H
B = BATCHES
S_LEN = SEQ
C = 16
TILES = S_LEN // C
QUAD = 32
NQ = P // QUAD
HPQ = H // NQ
GROUP = P // B
GROUPS = TILES // GROUP
PROJ = 4 * D + 2 * H
HALF = P // HD
L2_EPS = 1e-12
INV_COLS = H * C + 4 * H
ATT_COLS = H * C + H
SC_COLS = 4 * H


class Skew:

    def __init__(self, eng, n):
        self.eng, self.n = eng, n

    def do(self, stage, t):
        if isinstance(t.j, int) and not 0 <= t.j < self.n:
            return
        stage(t)

    def run(self, iteration, first, peel, end):
        stop = self.n - 6
        stop -= (stop - peel) % 2
        for k in range(first, peel):
            iteration(Step(0, k))
        with self.eng.Fori(0, (stop - peel) // 2) as i:
            for u in range(2):
                iteration(Step(i, peel + u))
        for k in range(stop, end):
            iteration(Step(0, k))


def tile_rows(t):
    return bass.ds(t.j, 1)


def project(nc, x, w, c, d):
    with Stage(nc) as ctx:
        def sb(name, shape, dt=F32):
            return ctx.enter_context(nc.sbuf_tensor("a_" + name, shape, dt))

        def pb(name, shape):
            return ctx.enter_context(nc.psum_tensor("a_" + name, shape, F32))

        raw = sb("raw", [P, KT, PROJ])
        w_h, w_l = sb("w_h", [P, KT, PROJ], F32R), sb("w_l", [P, KT, PROJ], F32R)
        xt, xn = sb("xt", [P, 2, D]), sb("xn", [P, 2, D])
        st, mv = sb("st", [P, 2, 6]), sb("mv", [P, 2, 2])
        sd, rs = sb("sd", [P, 2]), sb("rs", [P, 2])
        x_h, x_l = sb("x_h", [P, KT, P], F32R), sb("x_l", [P, KT, P], F32R)
        sq, mark = sb("sq", [P, 2 * D]), sb("mark", [P, 1])
        ss, nrm, rn = sb("ss", [P, 2 * H]), sb("nrm", [P, 2 * H]), sb("rn", [P, 2, 2 * H])
        tok = sb("tok", [P, 2, 4 * D])
        gate_logits = sb("ab", [P, 2, 2 * H])
        kqt = sb("kqt", [P, 2, 2 * B, 2, C])
        kbd = sb("kbd", [P, 2, 2, HALF, P])
        gram = sb("gram", [P, 2, 2 * D])
        ps_x, ps_qk, ps_vg = pb("ps_x", [P, 512]), pb("ps_qk", [P, 2, 512]), pb("ps_vg", [P, 512])
        ps_ab = pb("ps_ab", [P, 512])
        ps_t, ps_g = pb("ps_t", [P, 2, 2, P]), pb("ps_g", [P, 2, 512])

        wraw, wh, wl = (ctx.semaphore("a_" + n) for n in ("wraw", "wh", "wl"))
        with nc.Block() as block:
            @block.sync
            def _(sp):
                col = 0
                for a in w:
                    n = a.shape[1]
                    sp.dma_start(raw[:, :, col:col + n], a.rearrange("(k p) n -> p k n", p=P)).then_inc(wraw, 16)
                    col += n

            @block.scalar
            def _(act):
                act.wait_ge(wraw, 16 * len(w))
                act.activation(w_h[:], raw[:], ACT.Copy).then_inc(wh, 1)

            @block.vector
            def _(dve):
                dve.wait_ge(wraw, 16 * len(w))
                dve.wait_ge(wh, 1)
                dve.tensor_tensor(w_l[:], raw[:], w_h[:].bitcast(F32), ALU.subtract).then_inc(wl, 1)
                dve.wait_ge(wl, 1)

        names = ["x0", "x1", "mv", "sd", "rs", "cl", "chain", "xn", "xt", "xh", "xl", "qk", "vg", "sq", "ss", "nrm", "rn", "unit",
                 "vgs", "tqk", "kqt", "kbd0", "kbd1", "g", "gev", "tok0", "tok1", "ab0", "ab1", "gst0", "gst1"]
        s = {n: ctx.semaphore("a_" + n) for n in names}
        x_t = x.rearrange("(c p) d -> p c d", p=P)
        tok_t = d["tok"].rearrange("(c p) n -> p c n", p=P)
        ab_t = d["ab"].rearrange("(c b t) n -> c t b n", b=B, t=C)
        gram_t = d["gram"].rearrange("c (bh r) f -> c r bh f", bh=2)
        block = ctx.enter_context(nc.Block())

        @block.sync
        def _(sp):
            sk = Skew(sp, TILES)

            def load(t):
                at_least(sp, s["xn"], t.j - 1)
                sp.dma_start(xt[:, t.p:t.p + 1], x_t[:, tile_rows(t)]).then_inc(s[f"x{t.p}"], 16)

            def store(t):
                sp.wait_ge(s["unit"], t.j + 1)
                sp.wait_ge(s["vgs"], t.j + 1)
                sp.dma_start(tok_t[:, tile_rows(t)], tok[:, t.p:t.p + 1]).then_inc(s[f"tok{t.p}"], 16)
                sp.dma_start(ab_t[tile_rows(t)].rearrange("c t b n -> (c t) b n"), gate_logits[:, t.p]).then_inc(s[f"ab{t.p}"], 16)

            def store_gram(t):
                sp.wait_ge(s["gev"], t.j + 1)
                sp.dma_start(gram_t[tile_rows(t)].rearrange("a r bh f -> r (a bh) f"),
                             gram[:, t.p].rearrange("p (bh f) -> p bh f", bh=2)).then_inc(s[f"gst{t.p}"], 16)

            def iteration(t):
                sk.do(load, t.plus(2))
                sk.do(store, t.plus(-1))
                sk.do(store_gram, t.plus(-2))

            sk.run(iteration, -2, 4, TILES + 2)
            for p in range(2):
                for n in ("tok", "ab", "gst"):
                    sp.wait_ge(s[f"{n}{p}"], 16 * (TILES // 2))

        @block.tensor
        def _(pe):
            sk = Skew(pe, TILES)

            def transpose_x(t):
                pe.wait_ge(s["xn"], t.j + 1)
                at_least(pe, s["xl"], t.j)
                for k in range(KT):
                    last = pe.transpose(ps_x[:, k * P:(k + 1) * P], xn[:, t.p, k * P:(k + 1) * P], c["ident"][:])
                last.then_inc(s["xt"], 1)

            def products(t):
                pe.wait_ge(s["xh"], t.j + 1)
                pe.wait_ge(s["xl"], t.j + 1)
                at_least(pe, s["unit"], t.j - 1)
                at_least(pe, s["sq"], t.j - 1)
                at_least(pe, s["vgs"], t.j)
                for dst, col, n, sem in ((ps_qk[:, t.p], 0, 512, "qk"), (ps_vg[:], 512, 512, None),
                                         (ps_ab[:, 0:2 * H], 1024, 2 * H, "vg")):
                    m = 0
                    for xx, ww in ((x_h, w_h), (x_h, w_l), (x_l, w_h)):
                        for k in range(KT):
                            last = pe.matmul(dst, xx[:, k], ww[:, k, col:col + n], start=(m == 0), stop=(m == 5))
                            m += 1
                    if sem:
                        last.then_inc(s[sem], 1)

            def transpose_qk(t):
                pe.wait_ge(s["unit"], t.j + 1)
                at_least(pe, s["kqt"], t.j)
                for n in range(2):
                    for half in range(2):
                        col = (1 - n) * D + half * P
                        last = pe.transpose(ps_t[:, n, half], tok[:, t.p, col:col + P], c["ident"][:])
                last.then_inc(s["tqk"], 1)

            def chunk_products(t):
                pe.wait_ge(s["kqt"], t.j + 1)
                pe.wait_ge(s["kbd0"], t.j + 1)
                pe.wait_ge(s["kbd1"], t.j + 1)
                at_least(pe, s["gev"], t.j - 1)
                for b in range(B):
                    q, bh = b % NQ, b // NQ
                    for half in range(2):
                        last = pe.matmul(ps_g[q * QUAD:(q + 1) * QUAD, t.p, (2 * bh + half) * P:(2 * bh + half + 1) * P],
                                         kqt[:, t.p, half * B + b].rearrange("p n t -> p (n t)"),
                                         kbd[:, t.p, half, :, b * C:(b + 1) * C], start=True, stop=True)
                last.then_inc(s["g"], 1)

            def iteration(t):
                sk.do(products, t)
                sk.do(transpose_x, t.plus(1))
                sk.do(transpose_qk, t.plus(-1))
                sk.do(chunk_products, t.plus(-2))

            sk.run(iteration, -1, 4, TILES + 2)

        @block.scalar
        def _(act):
            sk = Skew(act, TILES)

            def std(t):
                act.wait_ge(s["mv"], t.j + 1)
                at_least(act, s["chain"], t.j - 1)
                act.activation(sd[:, t.p:t.p + 1], mv[:, t.p, 1:2], ACT.Sqrt, bias=c["eps"][:, 0:1]).then_inc(s["sd"], 1)

            def norms(t):
                act.wait_ge(s["ss"], t.j + 1)
                at_least(act, s["rn"], t.j)
                act.activation(nrm[:], ss[:], ACT.Sqrt).then_inc(s["nrm"], 1)

            def squares(t):
                act.wait_ge(s["qk"], t.j + 1)
                at_least(act, s["ss"], t.j)
                act.activation(sq[:], ps_qk[:, t.p], ACT.Square).then_inc(s["sq"], 1)

            def x_high(t):
                act.wait_ge(s["xt"], t.j + 1)
                at_least(act, s["vg"], t.j)
                act.activation(x_h[:], ps_x[:, 0:KT * P], ACT.Copy).then_inc(s["xh"], 1)

            def copy_rest(t):
                act.wait_ge(s["vg"], t.j + 1)
                at_least(act, s[f"tok{t.p}"], t.half * 16)
                at_least(act, s[f"ab{t.p}"], t.half * 16)
                act.activation(gate_logits[:, t.p], ps_ab[:, 0:2 * H], ACT.Copy)
                act.activation(tok[:, t.p, 2 * D:4 * D], ps_vg[:], ACT.Copy).then_inc(s["vgs"], 1)

            def copy_kq(t):
                act.wait_ge(s["tqk"], t.j + 1)
                at_least(act, s["g"], t.j - 1)
                at_least(act, s["kbd0"], t.j - 1)
                at_least(act, s["kbd1"], t.j - 1)
                for half in range(2):
                    last = act.activation(kqt[:, t.p, half * B:(half + 1) * B],
                                          ps_t[:, :, half].rearrange("p n (t b) -> p b n t", b=B), ACT.Copy)
                last.then_inc(s["kqt"], 1)

            def copy_gram(t):
                act.wait_ge(s["g"], t.j + 1)
                at_least(act, s[f"gst{t.p}"], t.half * 16)
                act.activation(gram[:, t.p], ps_g[:, t.p], ACT.Copy).then_inc(s["gev"], 1)

            def iteration(t):
                sk.do(std, t.plus(1))
                sk.do(norms, t.plus(-1))
                sk.do(squares, t)
                sk.do(x_high, t.plus(1))
                sk.do(copy_rest, t)
                sk.do(copy_kq, t.plus(-1))
                sk.do(copy_gram, t.plus(-2))

            sk.run(iteration, -1, 4, TILES + 2)

        @block.vector
        def _(dve):
            sk = Skew(dve, TILES)

            def moments(t):
                dve.wait_ge(s[f"x{t.p}"], (t.half + 1) * 16)
                at_least(dve, s["mv"], t.j - 1)
                at_least(dve, s["xn"], t.j - 1)
                dve.bn_stats(st[:, t.p], xt[:, t.p]).then_inc(s["chain"], 1)
                dve.wait_ge(s["chain"], t.j + 1)
                dve.tensor_copy(mark[:], st[:, t.p, 0:1])
                dve.bn_aggr(mv[:, t.p], st[:, t.p]).then_inc(s["mv"], 1)

            def normalise(t):
                dve.wait_ge(s["sd"], t.j + 1)
                dve.reciprocal(rs[:, t.p:t.p + 1], sd[:, t.p:t.p + 1]).then_inc(s["rs"], 1)
                dve.wait_ge(s["rs"], t.j + 1)
                at_least(dve, s["xt"], t.j - 1)
                dve.tensor_scalar(xn[:, t.p], xt[:, t.p], mv[:, t.p, 0:1], rs[:, t.p:t.p + 1],
                                  ALU.subtract, ALU.mult).then_inc(s["xn"], 1)

            def sums(t):
                dve.wait_ge(s["sq"], t.j + 1)
                at_least(dve, s["nrm"], t.j)
                dve.tensor_reduce(ss[:], sq[:].rearrange("p (h e) -> p h e", e=HD), AX.X, ALU.add).then_inc(s["ss"], 1)

            def unit(t):
                dve.wait_ge(s["nrm"], t.j + 1)
                at_least(dve, s["rn"], t.j)
                dve.tensor_scalar(rn[:, 0], nrm[:], L2_EPS, None, ALU.max).then_inc(s["cl"], 1)
                dve.wait_ge(s["cl"], t.j + 1)
                at_least(dve, s["unit"], t.j)
                dve.reciprocal(rn[:, 1], rn[:, 0]).then_inc(s["rn"], 1)
                dve.wait_ge(s["rn"], t.j + 1)
                at_least(dve, s[f"tok{t.p}"], t.half * 16)
                at_least(dve, s["tqk"], t.j - 1)
                for n in range(2):
                    last = dve.tensor_tensor(tok[:, t.p, (1 - n) * D:(2 - n) * D].rearrange("p (h e) -> p h e", e=HD),
                                             ps_qk[:, t.p, n * D:(n + 1) * D].rearrange("p (h e) -> p h e", e=HD),
                                             rn[:, 1, n * H:(n + 1) * H].unsqueeze(2).broadcast_to([P, H, HD]), ALU.mult)
                last.then_inc(s["unit"], 1)

            def x_low(t):
                dve.wait_ge(s["xh"], t.j + 1)
                at_least(dve, s["vg"], t.j)
                dve.tensor_tensor(x_l[:].rearrange("p k n -> p (k n)"), ps_x[:, 0:KT * P],
                                  x_h[:].bitcast(F32).rearrange("p k n -> p (k n)"), ALU.subtract).then_inc(s["xl"], 1)

            def spread0(t):
                dve.wait_ge(s["kqt"], t.j + 1)
                at_least(dve, s["g"], t.j - 1)
                dve.tensor_tensor(kbd[:, t.p, 0].rearrange("p h (b t) -> p h b t", b=B),
                                  kqt[:, t.p, 0:B, 0].unsqueeze(1).broadcast_to([P, HALF, B, C]),
                                  c["mask16"][:].unsqueeze(2).unsqueeze(3).broadcast_to([P, HALF, B, C]), ALU.mult).then_inc(s["kbd0"], 1)

            def iteration(t):
                sk.do(moments, t.plus(1))
                sk.do(sums, t.plus(-1))
                sk.do(normalise, t.plus(1))
                sk.do(unit, t.plus(-1))
                sk.do(x_low, t.plus(1))
                sk.do(spread0, t.plus(-1))

            
            
            sk.run(iteration, -1, 4, TILES + 2)

        @block.gpsimd
        def _(pool):
            sk = Skew(pool, TILES)

            def spread1(t):
                pool.wait_ge(s["kqt"], t.j + 1)
                at_least(pool, s["g"], t.j - 1)
                pool.tensor_tensor(kbd[:, t.p, 1].rearrange("p h (b t) -> p h b t", b=B),
                                   kqt[:, t.p, B:2 * B, 0].unsqueeze(1).broadcast_to([P, HALF, B, C]),
                                   c["mask16"][:].unsqueeze(2).unsqueeze(3).broadcast_to([P, HALF, B, C]), ALU.mult).then_inc(s["kbd1"], 1)

            sk.run(lambda t: sk.do(spread1, t.plus(-1)), -1, 4, TILES + 2)


def solve_chunks(nc, bias, c, d):
    with Stage(nc) as ctx:
        def sb(name, shape, dt=F32):
            return ctx.enter_context(nc.sbuf_tensor("b_" + name, shape, dt))

        kk_qk = sb("kk_qk", [P, 2, 2, C, H, C])
        ab = sb("ab", [P, 2, C, 2 * H])
        ab_bias = sb("bias", [P, 2 * H])
        gates = sb("gates", [P, C, 2 * H])
        neg_b = sb("neg_b", [P, C, H])
        decay = sb("decay", [P, C, H, C])
        inv_scal = sb("inv", [P, C, INV_COLS])
        att_g = sb("att", [P, C, ATT_COLS])
        inv = inv_scal[:, :, 0:H * C].rearrange("p j (h t) -> p j h t", h=H)
        att = att_g[:, :, 0:H * C].rearrange("p i (h t) -> p i h t", h=H)
        scal = inv_scal[:, :, H * C:INV_COLS]
        tmp = sb("tmp", [P, 8, H, 8])
        end_decay = sb("end_decay", [P, H])
        loaded = [ctx.semaphore(f"b_in{m}") for m in range(2)]
        names = ["bias", "init", "biased", "gates", "chain", "pchain", "ready", "pready", "out"]
        s = {n: ctx.semaphore("b_" + n) for n in names}
        block = ctx.enter_context(nc.Block())
        HV = 11

        @block.sync
        def _(sp):
            sp.dma_start(ab_bias[:], bias.partition_broadcast(P)).then_inc(s["bias"], 16)
            for g in range(GROUPS):
                if g >= 2:
                    sp.wait_ge(s["ready"], g - 1)
                    sp.wait_ge(s["pready"], g - 1)
                rows = slice(g * P, (g + 1) * P)
                sp.dma_start(kk_qk[:, g % 2].rearrange("p a t h i -> p (a t h i)"),
                             d["gram"].rearrange("c (b r) f -> (c b) (r f)", b=B)[rows]).then_inc(loaded[g % 2], 16)
                sp.dma_start(ab[:, g % 2].rearrange("p t h -> p (t h)"),
                             d["ab"].rearrange("(c t) n -> c (t n)", t=C)[rows]).then_inc(loaded[g % 2], 16)

        @block.scalar
        def _(act):
            for g in range(GROUPS):
                act.wait_ge(s["biased"], g + 1)
                act.activation(gates[:], ab[:, g % 2], ACT.Sigmoid).then_inc(s["gates"], 1)
                act.wait_ge(s["ready"], g + 1)
                act.wait_ge(s["pready"], g + 1)
                rows = slice(g * P, (g + 1) * P)
                act.dma_start(d["inv"][rows], inv_scal[:].rearrange("p j n -> p (j n)")).then_inc(s["out"], 16)
                act.dma_start(d["att"][rows], att_g[:].rearrange("p i n -> p (i n)")).then_inc(s["out"], 16)
                act.dma_start(d["end"].rearrange("q c (b m) -> c b q m", b=B)[g * GROUP:(g + 1) * GROUP]
                              .rearrange("c b q m -> (c b) q m"),
                              end_decay[:].rearrange("p (q m) -> p q m", q=NQ)).then_inc(s["out"], 16)
            act.wait_ge(s["out"], 48 * GROUPS)

        def heads(eng, sem, g, h0, h1, count):
            def then(ins):
                count[0] += 1
                ins.then_inc(s[sem], 1)
                eng.wait_ge(s[sem], count[0])

            n = h1 - h0
            hs = slice(h0, h1)
            kk, qk = kk_qk[:, g % 2, 0, :, hs], kk_qk[:, g % 2, 1, :, hs]
            al, be = gates[:, :, h0:h1], gates[:, :, H + h0:H + h1]
            dec, iv, at, nb = decay[:, :, hs], inv[:, :, hs], att[:, :, hs], neg_b[:, :, hs]
            eng.wait_ge(s["gates"], g + 1)
            if g:
                eng.wait_ge(s["out"], 48 * g)
            then(eng.tensor_scalar(nb, be, -1.0, None, ALU.mult))
            for t in range(1, C):
                then(eng.tensor_tensor(dec[:, t, :, 0:t], dec[:, t - 1, :, 0:t],
                                       al[:, t].unsqueeze(2).broadcast_to([P, n, t]), ALU.mult))
            for t in range(1, C):
                last = eng.tensor_tensor(kk[:, t], kk[:, t], dec[:, t - 1], ALU.mult)
            then(last)
            for t in range(1, C):
                last = eng.tensor_tensor(kk[:, t], kk[:, t], nb[:, t].unsqueeze(2).broadcast_to([P, n, C]), ALU.mult)
            then(last)
            for t in range(C):
                last = eng.tensor_tensor(at[:, :, :, t].rearrange("p i h -> p h i"), qk[:, t], dec[:, t], ALU.mult)
            sc = scal[:, :, h0:h1], scal[:, :, H + h0:H + h1], scal[:, :, 2 * H + h0:2 * H + h1], \
                scal[:, :, 3 * H + h0:3 * H + h1]
            then(eng.tensor_tensor(sc[1], dec[:, :, :, 0], al[:, 0:1].broadcast_to([P, C, n]), ALU.mult))
            eng.tensor_copy(sc[0][:, 0], nb[:, 0])
            eng.tensor_tensor(sc[0][:, 1:C], sc[1][:, 0:C - 1], nb[:, 1:C], ALU.mult)
            eng.tensor_copy(sc[2].rearrange("p t h -> p h t"), dec[:, C - 1])
            eng.tensor_copy(att_g[:, :, H * C + h0:H * C + h1], sc[1])
            eng.tensor_copy(end_decay[:, hs], sc[1][:, C - 1])
            eng.tensor_copy(sc[3], be)
            for t in range(1, C):
                last = eng.tensor_copy(iv[:, :, :, t].rearrange("p j h -> p h j"), kk[:, t])
            then(last)
            then(eng.memset(iv_first(iv, n), 0.0))
            for t in range(C):
                last = eng.memset(iv[:, t, :, t], 1.0)
            then(last)
            for i in range(1, C - 1):
                for j0 in range(0, i, 8):
                    j1 = min(j0 + 8, i)
                    for t0 in range(i + 1, C, 8):
                        t1 = min(t0 + 8, C)
                        nj, nt = j1 - j0, t1 - t0
                        for j in range(j0, j1):
                            last = eng.tensor_tensor(
                                tmp[:, j - j0, h0:h1, 0:nt], kk[:, t0:t1, :, i].rearrange("p t h -> p h t"),
                                iv[:, j, :, i].unsqueeze(2).broadcast_to([P, n, nt]), ALU.mult)
                        then(last)
                        then(eng.tensor_tensor(iv[:, j0:j1, :, t0:t1], iv[:, j0:j1, :, t0:t1],
                                               tmp[:, 0:nj, h0:h1, 0:nt], ALU.add))

        def iv_first(iv, n):
            return iv[:, 1:C, :, 0]

        @block.vector
        def _(dve):
            count = [0]
            dve.memset(decay[:], 0.0).then_inc(s["init"], 1)
            dve.wait_ge(s["init"], 1)
            for t in range(C):
                last = dve.memset(decay[:, t, :, t], 1.0)
            last.then_inc(s["init"], 1)
            dve.wait_ge(s["init"], 2)
            dve.wait_ge(s["bias"], 16)
            for g in range(GROUPS):
                dve.wait_ge(loaded[g % 2], 32 * (g // 2 + 1))
                dve.tensor_tensor(ab[:, g % 2], ab[:, g % 2], ab_bias[:].unsqueeze(1).broadcast_to([P, C, 2 * H]),
                                  ALU.add).then_inc(s["biased"], 1)
                heads(dve, "chain", g, 0, HV, count)
                dve.nop().then_inc(s["ready"], 1)
                dve.wait_ge(s["pready"], g + 1)

        @block.gpsimd
        def _(pool):
            count = [0]
            pool.wait_ge(s["init"], 2)
            for g in range(GROUPS):
                pool.wait_ge(loaded[g % 2], 32 * (g // 2 + 1))
                heads(pool, "pchain", g, HV, H, count)
                pool.nop().then_inc(s["pready"], 1)
                pool.wait_ge(s["ready"], g + 1)


def recur(nc, c, d):
    with Stage(nc) as ctx:
        def sb(name, shape, dt=F32):
            return ctx.enter_context(nc.sbuf_tensor("c_" + name, shape, dt))

        def pb(name, shape):
            return ctx.enter_context(nc.psum_tensor("c_" + name, shape, F32))

        BH = B // 2
        kv_in = sb("kv_in", [P, 2, 2, H, HD])
        inv_in = sb("inv_in", [P, 2, INV_COLS])
        q_in = sb("q_in", [P, 2, H, HD])
        g_in = sb("g_in", [P, 2, H])
        ka = sb("ka", [P, 2, 2, H * HD])
        kv = sb("kv", [P, 2, H, QUAD])
        gq = sb("gq", [P, 2, HPQ, NQ, QUAD])
        tbd = sb("tbd", [P, 2, B, H, C])
        kabd = sb("kabd", [P, 2, B, 2, H, HD])
        w_sb = sb("w_sb", [P, NQ, P])
        wu = sb("wu", [P, 2, NQ, NQ, QUAD])
        y_sb = sb("y_sb", [P, 2, HPQ, B, QUAD])
        ybd = sb("ybd", [P, 2, NQ, HPQ, B, QUAD])
        yt = sb("yt", [P, 2, HPQ, B, QUAD])
        s_sb = sb("s_sb", [P, B, P])
        state = sb("state", [P, 2, B, HPQ, HD])
        tmp = sb("tmp", [P, B, HPQ, HD])
        end_decay = sb("end_decay", [P, TILES, B * HPQ])
        ps_w, ps_wt = pb("ps_w", [P, NQ, P]), pb("ps_wt", [P, NQ, P])
        ps_y, ps_s, ps_st = pb("ps_y", [P, HPQ, B, QUAD]), pb("ps_s", [P, B, P]), pb("ps_st", [P, B, P])
        names = ["a_in0", "a_in1", "b_in0", "b_in1", "clear", "end", "tmpa", "tmp", "kv", "kd", "gq", "tbd", "kab_v",
                 "kab_s", "w", "wsb", "wt", "wu", "y", "ysb", "yt", "ybd0", "ybd1", "seq0", "seq1", "ss0", "ss1",
                 "st0", "st1", "s0", "s1", "out0", "out1"]
        s = {n: ctx.semaphore("c_" + n) for n in names}
        tok_t = d["tok"].rearrange("(c p) n -> p c n", p=P)
        inv_t = d["inv"].rearrange("(c b) (j n) -> c j b n", b=B, j=C)
        att_t = d["att"].rearrange("(c b) (j n) -> c j b n", b=B, j=C)
        o_t = d["o"].rearrange("c p n -> p c n")
        KAV = 5
        FIRST, PEEL, END = -5, 2, TILES
        block = ctx.enter_context(nc.Block())

        @block.sync
        def _(sp):
            sk = Skew(sp, TILES)
            sp.wait_ge(s["clear"], 1)
            for q in range(NQ):
                sp.dma_start(end_decay[q * QUAD:q * QUAD + HD],
                             d["end"][q].partition_broadcast(HD)).then_inc(s["end"], 16)

            def load_a(t):
                at_least(sp, s["kv"], t.j - 1)
                at_least(sp, s["kd"], t.j - 1)
                at_least(sp, s["tbd"], t.j - 1)
                sp.dma_start(kv_in[:, t.p:t.p + 1].rearrange("p a n h e -> p a (n h e)"),
                             tok_t[:, tile_rows(t), D:3 * D]).then_inc(s[f"a_in{t.p}"], 16)
                sp.dma_start(inv_in[:, t.p], inv_t[tile_rows(t)].rearrange("c j b n -> (c j) b n")).then_inc(s[f"a_in{t.p}"], 16)

            def load_b(t):
                at_least(sp, s["kab_v"], t.j - 1)
                at_least(sp, s["kab_s"], t.j - 1)
                at_least(sp, s["gq"], t.j - 1)
                rows = att_t[tile_rows(t)].rearrange("c j b n -> (c j) b n")
                sp.dma_start(g_in[:, t.p], rows[:, :, H * C:ATT_COLS]).then_inc(s[f"b_in{t.p}"], 16)
                sp.dma_start(q_in[:, t.p:t.p + 1].rearrange("p a h e -> p a (h e)"),
                             tok_t[:, tile_rows(t), 0:D]).then_inc(s[f"b_in{t.p}"], 16)
                sp.dma_start(ka[:, t.p, 1], rows[:, :, 0:H * C]).then_inc(s[f"b_in{t.p}"], 16)

            def spread_y(t):
                sp.wait_ge(s["ysb"], t.j + 1)
                at_least(sp, s["seq0"], t.j - 1)
                at_least(sp, s["seq1"], t.j - 1)
                for q in range(NQ):
                    rows = slice(q * QUAD, q * QUAD + HD)
                    sp.dma_start(ybd[rows, t.p, q], y_sb[rows, t.p]).then_inc(s[f"ybd{t.p}"], 16)

            def store(t):
                sp.wait_ge(s["s0"], t.j + 2)
                sp.wait_ge(s["s1"], t.j + 2)
                sp.dma_start(o_t[:, tile_rows(t)], state[:, 1 - t.p:2 - t.p].rearrange("p a b q e -> p a (b q e)")
                             ).then_inc(s[f"out{t.p}"], 16)

            def iteration(t):
                sk.do(load_b, t.plus(4))
                sk.do(load_a, t.plus(5))
                sk.do(store, t.plus(-1))
                sk.do(spread_y, t.plus(2))

            sk.run(iteration, FIRST, PEEL, END + 1)
            for p in range(2):
                sp.wait_ge(s[f"out{p}"], 16 * (TILES // 2))

        @block.tensor
        def _(pe):
            sk = Skew(pe, TILES)
            pe.wait_ge(s["clear"], 1)

            def solve(t):
                pe.wait_ge(s["kv"], t.j + 1)
                pe.wait_ge(s["tbd"], t.j + 1)
                at_least(pe, s["wsb"], t.j)
                for m in range(HPQ):
                    for q in range(NQ):
                        h = HPQ * q + m
                        last = pe.matmul(ps_w[q * QUAD:(q + 1) * QUAD, m], kv[:, t.p, h], tbd[:, t.p, :, h].rearrange("p b t -> p t b"),
                                         start=True, stop=True)
                last.then_inc(s["w"], 1)

            def solve_t(t):
                pe.wait_ge(s["wsb"], t.j + 1)
                at_least(pe, s["wu"], t.j)
                for m in range(HPQ):
                    last = pe.transpose(ps_wt[:, m], w_sb[:, m], c["ident"][:])
                last.then_inc(s["wt"], 1)

            def chunk(t):
                pe.wait_ge(s["wu"], t.j + 1)
                pe.wait_ge(s["gq"], t.j + 1)
                pe.wait_ge(s["kab_v"], t.j + 1)
                pe.wait_ge(s["kab_s"], t.j + 1)
                at_least(pe, s["ysb"], t.j)
                for m in range(HPQ):
                    pe.matmul(ps_y[:, m, :, HD:QUAD], gq[:, t.p, m].rearrange("p q x -> p (q x)"),
                              c["ident"][:].rearrange("p (t b) -> p b t", b=B), start=(m % 2 == 0), stop=False,
                              skip_group_check=True)
                    for q in range(NQ):
                        h = HPQ * q + m
                        last = pe.matmul(ps_y[q * QUAD:(q + 1) * QUAD, m], wu[:, t.p, m, q],
                                         kabd[:, t.p, :, :, h], start=False, stop=True, skip_group_check=True)
                last.then_inc(s["y"], 1)

            def advance(t, half):
                pe.wait_ge(s[f"s{half}"], t.j + 1)
                pe.wait_ge(s[f"ybd{t.p}"], (t.half + 1) * 16 * NQ)
                at_least(pe, s[f"ss{half}"], t.j)
                for b in range(half * BH, (half + 1) * BH):
                    for m in range(HPQ):
                        last = pe.matmul(ps_s[m * QUAD:m * QUAD + HD, b], state[:, t.p, b, m],
                                         ybd[:, t.p, :, m, b], start=True, stop=True)
                last.then_inc(s[f"seq{half}"], 1)

            def advance_t(t, half):
                pe.wait_ge(s[f"ss{half}"], t.j + 1)
                for b in range(half * BH, (half + 1) * BH):
                    last = pe.transpose(ps_st[:, b], s_sb[:, b], c["ident"][:])
                last.then_inc(s[f"st{half}"], 1)

            def iteration(t):
                sk.do(lambda u: advance(u, 0), t)
                sk.do(lambda u: advance(u, 1), t)
                sk.do(solve, t.plus(3))
                sk.do(lambda u: advance_t(u, 0), t)
                sk.do(lambda u: advance_t(u, 1), t)
                sk.do(solve_t, t.plus(3))
                sk.do(chunk, t.plus(2))

            sk.run(iteration, FIRST, PEEL, END)

        @block.scalar
        def _(act):
            sk = Skew(act, TILES)
            act.wait_ge(s["clear"], 1)

            def copy_s(t, half):
                act.wait_ge(s[f"seq{half}"], t.j + 1)
                at_least(act, s[f"st{half}"], t.j)
                bs = slice(half * BH, (half + 1) * BH)
                act.activation(s_sb[:, bs], ps_s[:, bs], ACT.Copy).then_inc(s[f"ss{half}"], 1)

            def copy_w(t):
                act.wait_ge(s["w"], t.j + 1)
                at_least(act, s["wt"], t.j)
                act.activation(w_sb[:], ps_w[:], ACT.Copy).then_inc(s["wsb"], 1)

            def copy_wu(t):
                act.wait_ge(s["wt"], t.j + 1)
                at_least(act, s["y"], t.j - 1)
                act.activation(wu[:, t.p].rearrange("p m q x -> p m (q x)"), ps_wt[:], ACT.Copy).then_inc(s["wu"], 1)

            def copy_y(t):
                act.wait_ge(s["y"], t.j + 1)
                at_least(act, s["yt"], t.j - 1)
                at_least(act, s[f"ybd{t.p}"], t.half * 16 * NQ)
                act.activation(y_sb[:, t.p], ps_y[:], ACT.Copy).then_inc(s["ysb"], 1)

            def spread_ka(t):
                act.wait_ge(s["kd"], t.j + 1)
                act.wait_ge(s[f"b_in{t.p}"], (t.half + 1) * 48)
                at_least(act, s["y"], t.j - 1)
                for b in range(KAV, B):
                    last = act.activation(kabd[:, t.p, b].rearrange("p n h e -> p (n h e)"),
                                          ka[:, t.p].rearrange("p n x -> p (n x)"), ACT.Copy,
                                          scale=c["mask_b"][:, b:b + 1])
                last.then_inc(s["kab_s"], 1)

            def iteration(t):
                sk.do(lambda u: copy_s(u, 0), t)
                sk.do(lambda u: copy_s(u, 1), t)
                sk.do(copy_w, t.plus(3))
                sk.do(spread_ka, t.plus(3))
                sk.do(copy_wu, t.plus(3))
                sk.do(copy_y, t.plus(2))

            sk.run(iteration, FIRST, PEEL, END)

        @block.vector
        def _(dve):
            sk = Skew(dve, TILES)
            dve.memset(end_decay[:], 0.0)
            dve.memset(ybd[:], 0.0)
            dve.memset(gq[:], 0.0)
            dve.memset(ps_s[:], 0.0)
            dve.memset(state[:, 0], 0.0).then_inc(s["clear"], 1)
            dve.wait_ge(s["clear"], 1)
            for half in range(2):
                dve.nop().then_inc(s[f"s{half}"], 1)

            def spread_inv(t):
                dve.wait_ge(s[f"a_in{t.p}"], (t.half + 1) * 32)
                at_least(dve, s["w"], t.j - 1)
                for b in range(B):
                    last = dve.tensor_scalar(tbd[:, t.p, b].rearrange("p h t -> p (h t)"), inv_in[:, t.p, 0:H * C],
                                             c["mask_b"][:, b:b + 1], None, ALU.mult)
                last.then_inc(s["tbd"], 1)

            def spread_ka(t):
                dve.wait_ge(s["kd"], t.j + 1)
                dve.wait_ge(s[f"b_in{t.p}"], (t.half + 1) * 48)
                at_least(dve, s["y"], t.j - 1)
                for b in range(KAV):
                    last = dve.tensor_scalar(kabd[:, t.p, b].rearrange("p n h e -> p (n h e)"),
                                             ka[:, t.p].rearrange("p n x -> p (n x)"),
                                             c["mask_b"][:, b:b + 1], None, ALU.mult)
                last.then_inc(s["kab_v"], 1)

            def next_state(t, half):
                dve.wait_ge(s[f"st{half}"], t.j + 1)
                dve.wait_ge(s["tmp"], t.j + 1)
                at_least(dve, s[f"out{t.p}"], t.half * 16)
                bs = slice(half * BH, (half + 1) * BH)
                dve.tensor_tensor(state[:, 1 - t.p, bs], ps_st[:, bs].rearrange("p b (m x) -> p b m x", m=HPQ)[:, :, :, 0:HD],
                                  tmp[:, bs], ALU.add).then_inc(s[f"s{half}"], 1)

            def turn_y(t):
                dve.wait_ge(s["ysb"], t.j + 1)
                at_least(dve, s["tmp"], t.j - 1)
                dve.transpose(yt[:, t.p].rearrange("p m b x -> p (m b x)"),
                              y_sb[:, t.p].rearrange("p m b x -> p (m b x)")).then_inc(s["yt"], 1)

            def iteration(t):
                sk.do(spread_ka, t.plus(3))
                sk.do(lambda u: next_state(u, 0), t)
                sk.do(lambda u: next_state(u, 1), t)
                sk.do(spread_inv, t.plus(4))
                sk.do(turn_y, t.plus(2))

            sk.run(iteration, FIRST, PEEL, END)

        @block.gpsimd
        def _(pool):
            sk = Skew(pool, TILES)
            pool.wait_ge(s["clear"], 1)
            pool.wait_ge(s["end"], 16 * NQ)

            def carry(t):
                pool.wait_ge(s["s0"], t.j + 1)
                pool.wait_ge(s["s1"], t.j + 1)
                pool.tensor_tensor(tmp[:].rearrange("p b m e -> p (b m) e"), state[:, t.p].rearrange("p b m e -> p (b m) e"),
                                   end_decay[:, tile_rows(t)].rearrange("p a n -> p (a n)").unsqueeze(2)
                                   .broadcast_to([P, B * HPQ, HD]), ALU.mult).then_inc(s["tmpa"], 1)
                pool.wait_ge(s["tmpa"], t.j + 1)
                pool.wait_ge(s["yt"], t.j + 1)
                pool.tensor_tensor(tmp[:], tmp[:], yt[:, t.p].rearrange("p m b x -> p b m x")[:, :, :, HD:QUAD],
                                   ALU.add).then_inc(s["tmp"], 1)

            def scale(dst, src, factor):
                return pool.tensor_tensor(dst, src, factor.unsqueeze(2).broadcast_to([P, H, HD]), ALU.mult)

            def token_scale(t):
                pool.wait_ge(s[f"a_in{t.p}"], (t.half + 1) * 32)
                at_least(pool, s["w"], t.j - 1)
                sc = inv_in[:, t.p, H * C:INV_COLS]
                scale(kv[:, t.p, :, 0:HD], kv_in[:, t.p, 0], sc[:, 0:H])
                scale(kv[:, t.p, :, HD:QUAD], kv_in[:, t.p, 1], sc[:, 3 * H:4 * H]).then_inc(s["kv"], 1)
                at_least(pool, s["kab_v"], t.j - 1)
                at_least(pool, s["kab_s"], t.j - 1)
                scale(ka[:, t.p, 0].rearrange("p (h e) -> p h e", h=H), kv_in[:, t.p, 0],
                      sc[:, 2 * H:3 * H]).then_inc(s["kd"], 1)

            def query_scale(t):
                pool.wait_ge(s[f"b_in{t.p}"], (t.half + 1) * 48)
                at_least(pool, s["y"], t.j - 1)
                pool.tensor_tensor(gq[:, t.p].rearrange("p m q x -> p q m x")[:, :, :, 0:HD],
                                   q_in[:, t.p].rearrange("p (q m) e -> p q m e", m=HPQ),
                                   g_in[:, t.p].rearrange("p (q m) -> p q m", m=HPQ).unsqueeze(3)
                                   .broadcast_to([P, NQ, HPQ, HD]), ALU.mult).then_inc(s["gq"], 1)

            def iteration(t):
                sk.do(carry, t)
                sk.do(token_scale, t.plus(4))
                sk.do(query_scale, t.plus(3))

            sk.run(iteration, FIRST, PEEL, END)


def output(nc, x, dst, wo, g_norm, c, d):
    with Stage(nc) as ctx:
        def sb(name, shape, dt=F32):
            return ctx.enter_context(nc.sbuf_tensor("d_" + name, shape, dt))

        raw, gn = sb("raw", [P, KT, D]), sb("gn", [P, KT])
        w_h, w_l = sb("w_h", [P, KT, D], F32R), sb("w_l", [P, KT, D], F32R)
        o_in = sb("o_in", [P, 2, 2, D])
        gate, xt = sb("gate", [P, 2, 2, D]), sb("xt", [P, 2, 2, D])
        sig = sb("sig", [P, 2, D])
        sq, ss, rstd = sb("sq", [P, D]), sb("ss", [P, 2, 2]), sb("rstd", [P, 2, 2])
        y, res = sb("y", [P, 2, 2, D]), sb("res", [P, 2, 2, D])
        y_h, y_l = sb("y_h", [P, 2, KT, P], F32R), sb("y_l", [P, 2, KT, P], F32R)
        ps_t = ctx.enter_context(nc.psum_tensor("d_ps_t", [P, 2, 2, KT, P], F32))
        ps_o = ctx.enter_context(nc.psum_tensor("d_ps_o", [P, 2, 2, D], F32))
        names = ["raw", "wg", "wh", "wl", "in0", "in1", "x0", "x1", "sq", "ms", "rstd", "silu", "y", "yt", "yh", "yl", "o", "sum",
                 "out0", "out1"]
        s = {n: ctx.semaphore("d_" + n) for n in names}
        x_t = x.rearrange("(c p) d -> p c d", p=P)
        out_t = dst.rearrange("(c p) d -> p c d", p=P)
        tok_t = d["tok"].rearrange("(c p) n -> p c n", p=P)
        o_t = d["o"].rearrange("c (q z t) (b m) -> c z (t b) q m", q=NQ, z=2, b=B)
        PAIRS_T = TILES // 2
        IN = 16 * 3
        FIRST, PEEL, END = -3, 3, PAIRS_T + 1
        block = ctx.enter_context(nc.Block())

        def two(t):
            return bass.ds(t.j * 2, 2)

        @block.sync
        def _(sp):
            sk = Skew(sp, PAIRS_T)
            sp.dma_start(raw[:], wo.rearrange("(k p) n -> p k n", p=P)).then_inc(s["raw"], 16)
            sp.dma_start(gn[:], g_norm).then_inc(s["raw"], 16)

            def load(t):
                at_least(sp, s["y"], t.j - 1)
                for u in range(2):
                    sp.dma_start(o_in[:, t.p, u].rearrange("p (q m) -> p q m", q=NQ),
                                 o_t[bass.ds(t.j * 2 + u, 1), 1].rearrange("c p q m -> (c p) q m")
                                 ).then_inc(s[f"in{t.p}"], 16)
                sp.dma_start(gate[:, t.p], tok_t[:, two(t), 3 * D:4 * D]).then_inc(s[f"in{t.p}"], 16)

            def load_x(t):
                at_least(sp, s["sum"], t.j - 1)
                sp.dma_start(xt[:, t.p], x_t[:, two(t)]).then_inc(s[f"x{t.p}"], 16)

            def iteration(t):
                sk.do(load, t.plus(3))
                sk.do(load_x, t.plus(1))

            sk.run(iteration, FIRST, PEEL, END)

        @block.scalar
        def _(act):
            sk = Skew(act, PAIRS_T)
            act.wait_ge(s["wg"], 1)
            act.activation(w_h[:], raw[:], ACT.Copy).then_inc(s["wh"], 1)

            def squares(t):
                act.wait_ge(s[f"in{t.p}"], (t.half + 1) * IN)
                at_least(act, s["rstd"], t.j - 1)
                at_least(act, s["y"], t.j)
                for u in range(2):
                    if u:
                        act.wait_ge(s["sq"], t.j * 2 + 1)
                    else:
                        at_least(act, s["sq"], t.j * 2)
                    act.activation(sq[:], o_in[:, t.p, u], ACT.Square,
                                   accum_out=ss[:, t.p, u:u + 1]).then_inc(s["sq"], 1)
                act.activation(sig[:], gate[:, t.p], ACT.Silu).then_inc(s["silu"], 1)

            def high(t):
                act.wait_ge(s["yt"], t.j + 1)
                at_least(act, s["o"], t.j)
                act.activation(y_h[:], ps_t[:, t.p], ACT.Copy).then_inc(s["yh"], 1)

            def store(t):
                act.wait_ge(s["sum"], t.j + 1)
                act.dma_start(out_t[:, two(t)], res[:, t.p]).then_inc(s[f"out{t.p}"], 16)

            def iteration(t):
                sk.do(high, t)
                sk.do(squares, t.plus(1))
                sk.do(store, t.plus(-1))

            sk.run(iteration, FIRST, PEEL, END)
            for p in range(2):
                act.wait_ge(s[f"out{p}"], 16 * (PAIRS_T // 2))

        @block.gpsimd
        def _(pool):
            sk = Skew(pool, PAIRS_T)

            def power(t):
                pool.wait_ge(s["ms"], t.j + 1)
                at_least(pool, s["sum"], t.j - 1)
                pool.tensor_tensor(rstd[:, t.p], ss[:, t.p], c["minus_half"][:], ALU.pow).then_inc(s["rstd"], 1)

            sk.run(lambda t: sk.do(power, t.plus(1)), FIRST, PEEL, END)

        @block.vector
        def _(dve):
            sk = Skew(dve, PAIRS_T)
            dve.memset(ss[:], 0.0)
            dve.wait_ge(s["raw"], 32)
            for k in range(KT):
                last = dve.tensor_scalar(raw[:, k], raw[:, k], gn[:, k:k + 1], None, ALU.mult)
            last.then_inc(s["wg"], 1)
            dve.wait_ge(s["wh"], 1)
            dve.tensor_tensor(w_l[:], raw[:], w_h[:].bitcast(F32), ALU.subtract).then_inc(s["wl"], 1)

            def gated(t):
                dve.wait_ge(s["sq"], t.j * 2 + 2)
                dve.tensor_scalar(ss[:, t.p], ss[:, t.p], 1.0 / D, EPS, ALU.mult, ALU.add).then_inc(s["ms"], 1)
                dve.wait_ge(s["silu"], t.j + 1)
                at_least(dve, s["yt"], t.j - 1)
                dve.tensor_tensor(y[:, t.p], o_in[:, t.p], sig[:], ALU.mult).then_inc(s["y"], 1)

            def low(t):
                dve.wait_ge(s["yh"], t.j + 1)
                at_least(dve, s["o"], t.j)
                dve.tensor_tensor(y_l[:], ps_t[:, t.p], y_h[:].bitcast(F32), ALU.subtract).then_inc(s["yl"], 1)

            def add(t):
                dve.wait_ge(s["o"], t.j + 1)
                dve.wait_ge(s["rstd"], t.j + 1)
                dve.wait_ge(s[f"x{t.p}"], (t.half + 1) * 16)
                at_least(dve, s[f"out{t.p}"], t.half * 16)
                for u in range(2):
                    last = dve.scalar_tensor_tensor(res[:, t.p, u], ps_o[:, t.p, u], rstd[:, t.p, u:u + 1], xt[:, t.p, u],
                                                    ALU.mult, ALU.add)
                last.then_inc(s["sum"], 1)

            def iteration(t):
                sk.do(low, t)
                sk.do(gated, t.plus(1))
                sk.do(add, t.plus(-1))

            sk.run(iteration, FIRST, PEEL, END)

        @block.tensor
        def _(pe):
            sk = Skew(pe, PAIRS_T)
            pe.wait_ge(s["wl"], 1)

            def turn(t):
                pe.wait_ge(s["y"], t.j + 1)
                at_least(pe, s["yl"], t.j - 1)
                for u in range(2):
                    for k in range(KT):
                        last = pe.transpose(ps_t[:, t.p, u, k], y[:, t.p, u, k * P:(k + 1) * P], c["ident"][:])
                last.then_inc(s["yt"], 1)

            def product(t):
                pe.wait_ge(s["yh"], t.j + 1)
                pe.wait_ge(s["yl"], t.j + 1)
                at_least(pe, s["sum"], t.j - 1)
                for u in range(2):
                    m = 0
                    for yy, ww in ((y_h, w_h), (y_h, w_l), (y_l, w_h)):
                        for k in range(KT):
                            last = pe.matmul(ps_o[:, t.p, u], yy[:, u, k], ww[:, k], start=(m == 0), stop=(m == 5))
                            m += 1
                last.then_inc(s["o"], 1)

            def iteration(t):
                sk.do(turn, t.plus(1))
                sk.do(product, t)

            sk.run(iteration, FIRST, PEEL, END)


CONSTANTS = {
    "ident": ([P, P], lambda: np.eye(P)),
    "before": ([P, P], lambda: np.triu(np.ones((P, P)), 1)),
    "ones": ([P, P], lambda: np.ones((P, P))),
    "iota_e": ([P, E], lambda: np.tile(np.arange(E), (P, 1))),
    "iota_128": ([P, PAIRS], lambda: np.tile(np.arange(PAIRS) * P, (P, 1))),
    "iota_tile": ([1, SLOT_TILES], lambda: np.arange(SLOT_TILES)[None]),
    "dump_row": ([P, PAIRS], lambda: SLOTS + np.arange(PAIRS)[None] * P + np.arange(P)[:, None]),
    "eps": ([P, 1], lambda: np.full((P, 1), EPS)),
    "minus_half": ([P, 2], lambda: np.full((P, 2), -0.5)),
    "mask_b": ([P, B], lambda: np.arange(P)[:, None] % B == np.arange(B)[None]),
    "mask16": ([P, HALF], lambda: np.arange(P)[:, None] // HD == np.arange(HALF)[None]),
}


def layer(nc, t, out):
    with Stage(nc) as ctx:
        def dram(name, shape):
            return nc.dram_tensor(name, shape, F32, kind="Internal").ap()

        x = t["x"]
        x1 = dram("x_after_first", [SEQ * BATCHES, D])
        slots = dict(xs=dram("slot_rows", [SLOTS + DUMP, D]), ys=dram("slot_results", [SLOTS, D]))
        scratch = dict(tok=dram("projections", [SEQ * BATCHES, 4 * D]), ab=dram("decay_logits", [SEQ * BATCHES, 2 * H]),
                       gram=dram("chunk_products", [TILES, 2 * B * C, H * C]),
                       inv=dram("inverses", [TILES * B, C * INV_COLS]), att=dram("masked_qk", [TILES * B, C * ATT_COLS]),
                       end=dram("end_decays", [NQ, TILES, B * HPQ]), o=dram("states", [TILES, P, B * D // NQ]))
        consts = {k: ctx.enter_context(nc.sbuf_tensor(f"const_{k}_sb", shape, F32)) for k, (shape, _) in CONSTANTS.items()}
        slots["pos_gather"] = ctx.enter_context(nc.sbuf_tensor("pos_gather", [P, PAIRS], I32))
        slots["pos_scatter"] = ctx.enter_context(nc.sbuf_tensor("pos_scatter", [P, PAIRS], I32))
        slots["half_w"] = ctx.enter_context(nc.sbuf_tensor("half_w", [P, PAIRS], F32))
        slots["tile_expert"] = ctx.enter_context(nc.sbuf_tensor("tile_expert", [1, SLOT_TILES], I32))
        copied = ctx.semaphore("rest_copied")
        consts_in = ctx.semaphore("consts_in")
        with nc.Block() as block:
            @block.sync
            def _(sp):
                for k in consts:
                    sp.dma_start(consts[k][:], t["const_" + k]).then_inc(consts_in, 16)
                sp.dma_start(x1.rearrange("(n b) d -> n b d", b=B)[:, FFN_BATCHES:B],
                             x.rearrange("(n b) d -> n b d", b=B)[:, FFN_BATCHES:B]).then_inc(copied, 16)
                sp.wait_ge(consts_in, 16 * len(consts))

        expert_w = (t["w1a_t"], t["w1b"], t["w2a_t"], t["w2b"])
        routing(nc, t["expert_indices"], t["expert_weights"], consts, slots)
        ffn_scatter(nc, "fs1", x, consts, slots)
        ffn_experts(nc, "fe1", expert_w, consts, slots)
        ffn_combine(nc, "fc1", x, x1, consts, slots)
        with nc.Block() as block:
            @block.sync
            def _(sp):
                sp.wait_ge(copied, 16)

        project(nc, x1, [t[n] for n in ("wk", "wq", "wv", "wg", "wa", "wb")], consts, scratch)
        solve_chunks(nc, t["gate_bias"], consts, scratch)
        recur(nc, consts, scratch)
        output(nc, x1, out, t["wo"], t["g_norm"], consts, scratch)
        ffn_scatter(nc, "fs2", out, consts, slots)
        ffn_experts(nc, "fe2", expert_w, consts, slots)
        ffn_combine(nc, "fc2", out, out, consts, slots)


def kernel(L0_attn_x, L0_attn_Wq, L0_attn_Wk, L0_attn_Wv, L0_attn_Wa, L0_attn_ba, L0_attn_Wb, L0_attn_bb, L0_attn_Wg,
           L0_attn_Wo, L0_attn_g_norm, L0_ffn_expert_weights, L0_ffn_expert_indices, L0_ffn_w1_A, L0_ffn_w1_B,
           L0_ffn_w2_A, L0_ffn_w2_B):
    import concourse.bacc as bacc
    from concourse.bass_utils import run_bass_kernel_spmd

    def in_tiles(a, batches):
        a = np.asarray(a)
        return a.reshape(batches, SEQ, a.shape[-1]).transpose(1, 0, 2).reshape(batches * SEQ, a.shape[-1])

    arrays = {
        "x": in_tiles(L0_attn_x, BATCHES),
        "wk": L0_attn_Wk, "wq": L0_attn_Wq, "wv": L0_attn_Wv, "wg": L0_attn_Wg, "wa": L0_attn_Wa, "wb": L0_attn_Wb,
        "gate_bias": np.concatenate([np.asarray(L0_attn_ba), np.asarray(L0_attn_bb)]),
        "wo": L0_attn_Wo, "g_norm": np.asarray(L0_attn_g_norm).reshape(KT, P).T,
        "expert_weights": in_tiles(L0_ffn_expert_weights, FFN_BATCHES),
        "expert_indices": in_tiles(L0_ffn_expert_indices, FFN_BATCHES),
        "w1a_t": np.asarray(L0_ffn_w1_A).T, "w1b": L0_ffn_w1_B, "w2a_t": np.asarray(L0_ffn_w2_A).T, "w2b": L0_ffn_w2_B,
    }
    for name, (_, value) in CONSTANTS.items():
        arrays["const_" + name] = value().astype(np.float32)
    arrays = {name: np.ascontiguousarray(a) for name, a in arrays.items()}
    nc = bacc.Bacc("TRN2", target_bir_lowering=False, num_devices=1)
    tensors = {name: nc.dram_tensor(name, a.shape, mybir.dt.from_np(a.dtype), kind="ExternalInput").ap()
               for name, a in arrays.items()}
    out = nc.dram_tensor("out", (SEQ * BATCHES, D), F32, kind="ExternalOutput").ap()
    layer(nc, tensors, out)
    result = run_bass_kernel_spmd(nc, [arrays], core_ids=[0]).results[0]["out"]
    return result.reshape(SEQ, BATCHES, D).transpose(1, 0, 2)
```

```python
from contextlib import ExitStack

import concourse.bass as bass
import numpy as np
from concourse import mybir

F32 = mybir.dt.float32
F32R = mybir.dt.float32r
I32 = mybir.dt.int32
ALU = mybir.AluOpType
ACT = mybir.ActivationFunctionType
AX = mybir.AxisListType

P = 128
D = 256
KT = D // P
EPS = 1e-5

T_FFN = 2048
BATCHES = 8
SEQ = 1024
FFN_BATCHES = T_FFN // SEQ
TOPK = 2
E = 8
RANK = 64
FF = 1024
FT = FF // P
TT = T_FFN // P
PAIRS = TT * TOPK
SLOT_TILES = 40
SLOTS = SLOT_TILES * P
PEELED = 4
DUMP = T_FFN * TOPK


class Step:

    def __init__(self, i, off):
        self.i, self.off = i, off
        self.p = off % 2
        self.j = i * 2 + off
        self.half = i + off // 2

    def plus(self, n):
        return Step(self.i, self.off + n)


class Stage(ExitStack):

    def __init__(self, nc):
        super().__init__()
        self.nc, self.held = nc, []

    def semaphore(self, name):
        self.held.append(self.nc.alloc_semaphore(name))
        return self.held[-1]

    def __exit__(self, *exc):
        done = super().__exit__(*exc)
        if self.held and exc[0] is None:
            self.nc.clear_and_free_semaphores(self.held)
            self.nc.all_engine_barrier()
        return done


def at_least(eng, sem, n):
    if isinstance(n, int):
        if n > 0:
            eng.wait_ge(sem, n)
        return
    assert n.min_val > 0
    eng.wait_ge(sem, n)


class Skew:

    def __init__(self, eng, n):
        self.eng, self.n = eng, n

    def do(self, stage, t):
        if isinstance(t.j, int) and not 0 <= t.j < self.n:
            return
        stage(t)

    def run(self, iteration, first, peel, end):
        stop = self.n - 6
        stop -= (stop - peel) % 2
        for k in range(first, peel):
            iteration(Step(0, k))
        with self.eng.Fori(0, (stop - peel) // 2) as i:
            for u in range(2):
                iteration(Step(i, peel + u))
        for k in range(stop, end):
            iteration(Step(0, k))


def routing(nc, expert_indices, expert_weights, c, rt):
    with Stage(nc) as ctx:
        idx_i = ctx.enter_context(nc.sbuf_tensor("idx_i", [P, PAIRS], I32))
        idx_f = ctx.enter_context(nc.sbuf_tensor("idx_f", [P, PAIRS], F32))
        wts = ctx.enter_context(nc.sbuf_tensor("wts", [P, PAIRS], F32))
        onehot = ctx.enter_context(nc.sbuf_tensor("onehot", [P, PAIRS, E], F32))
        upto = ctx.enter_context(nc.sbuf_tensor("upto", [P, PAIRS, E], F32))
        place = ctx.enter_context(nc.sbuf_tensor("place", [P, PAIRS, E], F32))
        ones_pe = ctx.enter_context(nc.sbuf_tensor("ones_pe", [P, PAIRS], F32))
        cmp = ctx.enter_context(nc.sbuf_tensor("cmp", [P, E, PAIRS], F32))
        cmp2 = ctx.enter_context(nc.sbuf_tensor("cmp2", [1, SLOT_TILES, E], F32))
        ntile = ctx.enter_context(nc.sbuf_tensor("ntile", [P, E], F32))
        endt = ctx.enter_context(nc.sbuf_tensor("endt", [P, E], F32))
        base = ctx.enter_context(nc.sbuf_tensor("base", [P, E], F32))
        texp_f = ctx.enter_context(nc.sbuf_tensor("texp_f", [1, SLOT_TILES], F32))
        pos_f = ctx.enter_context(nc.sbuf_tensor("pos_f", [P, PAIRS], F32))
        valid = ctx.enter_context(nc.sbuf_tensor("valid", [P, PAIRS], F32))
        zero_rows = ctx.enter_context(nc.sbuf_tensor("zero_rows", [P, 10 * D], F32))
        ps_within = ctx.enter_context(nc.psum_tensor("ps_within", [P, PAIRS * E], F32))
        ps_total = ctx.enter_context(nc.psum_tensor("ps_total", [P, PAIRS * E], F32))
        loaded = ctx.semaphore("r_loaded")
        onehot_ready = ctx.semaphore("r_onehot")
        counts_ready = ctx.semaphore("r_counts")
        chain = ctx.semaphore("r_chain")
        zero_ready = ctx.semaphore("r_zero")
        cleared = ctx.semaphore("r_cleared")
        block = ctx.enter_context(nc.Block())

        @block.sync
        def _(sp):
            sp.dma_start(idx_i[:].rearrange("p (i k) -> p i k", k=TOPK),
                         expert_indices.rearrange("(i p) k -> p i k", p=P)).then_inc(loaded, 16)
            sp.dma_start(wts[:].rearrange("p (i k) -> p i k", k=TOPK),
                         expert_weights.rearrange("(i p) k -> p i k", p=P)).then_inc(loaded, 16)
            sp.wait_ge(zero_ready, 1)
            for n in range(SLOT_TILES // 10):
                sp.dma_start(rt["xs"][n * 10 * P:(n + 1) * 10 * P, :].rearrange("(p r) d -> p (r d)", r=10),
                             zero_rows[:]).then_inc(cleared, 16)
            sp.wait_ge(cleared, 16 * (SLOT_TILES // 10))

        @block.gpsimd
        def _(pool):
            pool.memset(zero_rows[:], 0.0).then_inc(zero_ready, 1)

        @block.tensor
        def _(pe):
            pe.wait_ge(onehot_ready, 1)
            pe.matmul(ps_within[:], c["before"][:], onehot[:].rearrange("p a e -> p (a e)"), start=True, stop=True)
            pe.matmul(ps_total[:], c["ones"][:], onehot[:].rearrange("p a e -> p (a e)"),
                      start=True, stop=True).then_inc(counts_ready, 1)

        @block.vector
        def _(dve):
            n = [0]

            def then(ins):
                n[0] += 1
                ins.then_inc(chain, 1)
                dve.wait_ge(chain, n[0])

            dve.wait_ge(loaded, 32)
            then(dve.tensor_copy(idx_f[:], idx_i[:]))
            dve.memset(ones_pe[:], 1.0)
            dve.tensor_tensor(onehot[:], idx_f[:].unsqueeze(2).broadcast_to([P, PAIRS, E]),
                              c["iota_e"][:].unsqueeze(1).broadcast_to([P, PAIRS, E]),
                              ALU.is_equal).then_inc(onehot_ready, 1)
            dve.wait_ge(counts_ready, 1)
            tot = ps_total[:].rearrange("p (a e) -> p a e", e=E)
            within = ps_within[:].rearrange("p (a e) -> p a e", e=E)
            for e in range(E):
                last = dve.tensor_tensor_scan(upto[:, :, e], ones_pe[:], tot[:, :, e], 0.0, ALU.mult, ALU.add)
            then(last)
            then(dve.tensor_tensor(cmp[:], upto[:, PAIRS - 1, :].unsqueeze(2).broadcast_to([P, E, PAIRS]),
                                   c["iota_128"][:].unsqueeze(1).broadcast_to([P, E, PAIRS]), ALU.is_gt))
            then(dve.tensor_reduce(ntile[:], cmp[:], AX.X, ALU.add))
            then(dve.tensor_tensor_scan(endt[:], ones_pe[:, 0:E], ntile[:], 0.0, ALU.mult, ALU.add))
            then(dve.tensor_tensor(base[:], endt[:], ntile[:], ALU.subtract))
            then(dve.tensor_scalar(base[:], base[:], float(P), None, ALU.mult))
            then(dve.tensor_tensor(upto[:], upto[:], tot, ALU.subtract))
            then(dve.tensor_tensor(place[:], upto[:], within, ALU.add))
            then(dve.tensor_tensor(place[:], place[:], base[:].unsqueeze(1).broadcast_to([P, PAIRS, E]), ALU.add))
            then(dve.tensor_tensor(place[:], place[:], onehot[:], ALU.mult))
            then(dve.tensor_reduce(pos_f[:], place[:], AX.X, ALU.add))
            then(dve.tensor_reduce(valid[:], onehot[:], AX.X, ALU.add))
            then(dve.tensor_copy(rt["pos_gather"][:], pos_f[:]))
            then(dve.tensor_tensor(wts[:], wts[:], valid[:], ALU.mult))
            then(dve.tensor_scalar(rt["half_w"][:], wts[:], 0.5, None, ALU.mult))
            then(dve.tensor_scalar(valid[:], valid[:], -1.0, 1.0, ALU.mult, ALU.add))
            then(dve.tensor_tensor(valid[:], valid[:], c["dump_row"][:], ALU.mult))
            then(dve.tensor_tensor(pos_f[:], pos_f[:], valid[:], ALU.add))
            then(dve.tensor_copy(rt["pos_scatter"][:], pos_f[:]))
            then(dve.tensor_tensor(cmp2[:], endt[0:1, :].unsqueeze(1).broadcast_to([1, SLOT_TILES, E]),
                                   c["iota_tile"][:].unsqueeze(2).broadcast_to([1, SLOT_TILES, E]), ALU.is_le))
            then(dve.tensor_reduce(texp_f[:], cmp2[:], AX.X, ALU.add))
            then(dve.tensor_scalar(texp_f[:], texp_f[:], float(E - 1), None, ALU.min))
            then(dve.tensor_copy(rt["tile_expert"][:], texp_f[:]))


def ffn_rows(a):
    return a.rearrange("(i r b) d -> i r b d", r=P // FFN_BATCHES, b=BATCHES)[:, :, 0:FFN_BATCHES]


def scatter_programs(nc, ctx, name, src, c, rt):
    xt = ctx.enter_context(nc.sbuf_tensor(f"{name}_x", [P, 4, D], F32))
    xn = ctx.enter_context(nc.sbuf_tensor(f"{name}_xn", [P, 4, D], F32))
    st = ctx.enter_context(nc.sbuf_tensor(f"{name}_st", [P, 4, 6], F32))
    mv = ctx.enter_context(nc.sbuf_tensor(f"{name}_mv", [P, 4, 2], F32))
    sd = ctx.enter_context(nc.sbuf_tensor(f"{name}_sd", [P, 4], F32))
    rs = ctx.enter_context(nc.sbuf_tensor(f"{name}_rs", [P, 4], F32))
    in0 = ctx.semaphore(f"{name}_in0")
    in1 = ctx.semaphore(f"{name}_in1")
    in2 = ctx.semaphore(f"{name}_in2")
    in3 = ctx.semaphore(f"{name}_in3")
    var_ready = ctx.semaphore(f"{name}_var")
    std_ready = ctx.semaphore(f"{name}_std")
    norm_ready = ctx.semaphore(f"{name}_norm")
    chain = ctx.semaphore(f"{name}_chain")
    out0 = ctx.semaphore(f"{name}_out0")
    out1 = ctx.semaphore(f"{name}_out1")
    out2 = ctx.semaphore(f"{name}_out2")
    out3 = ctx.semaphore(f"{name}_out3")
    row_in, row_out = [in0, in1, in2, in3], [out0, out1, out2, out3]
    src_t = ffn_rows(src)

    def scatter_sync(sp, i):
        if i >= 4:
            sp.wait_ge(norm_ready, i - 3)
        sp.dma_start(xt[:, i % 4], src_t[i]).then_inc(row_in[i % 4], 16)

    def scatter_scalar(act, i):
        act.wait_ge(var_ready, i + 1)
        act.activation(sd[:, i % 4:i % 4 + 1], mv[:, i % 4, 1:2], ACT.Sqrt,
                       bias=c["eps"][:, 0:1]).then_inc(std_ready, 1)

    def scatter_vector(dve, between):
        n = [0]

        def then(ins):
            n[0] += 1
            ins.then_inc(chain, 1)
            dve.wait_ge(chain, n[0])

        def moments(i):
            dve.wait_ge(row_in[i % 4], 16 * (i // 4 + 1))
            if i >= 4:
                dve.wait_ge(var_ready, i - 3)
            then(dve.bn_stats(st[:, i % 4], xt[:, i % 4]))
            dve.bn_aggr(mv[:, i % 4], st[:, i % 4]).then_inc(var_ready, 1)

        def normalise(i):
            dve.wait_ge(std_ready, i + 1)
            then(dve.reciprocal(rs[:, i % 4:i % 4 + 1], sd[:, i % 4:i % 4 + 1]))
            if i >= 4:
                dve.wait_ge(row_out[i % 4], 32 * (i // 4))
            dve.tensor_scalar(xn[:, i % 4], xt[:, i % 4], mv[:, i % 4, 0:1], rs[:, i % 4:i % 4 + 1],
                              ALU.subtract, ALU.mult).then_inc(norm_ready, 1)

        moments(0)
        for i in range(TT):
            if i + 1 < TT:
                if i >= 3:
                    dve.wait_ge(norm_ready, i - 2)
                moments(i + 1)
            normalise(i)
            between(i)

    def scatter_gpsimd(pool):
        for i in range(TT):
            pool.wait_ge(norm_ready, i + 1)
            for k in range(TOPK):
                col = i * TOPK + k
                pool.indirect_dma_start(
                    rt["xs"], bass.IndirectOffsetOnAxis(ap=rt["pos_scatter"][:, col:col + 1], axis=0),
                    xn[:, i % 4], None).then_inc(row_out[i % 4], 16)
        for m in range(4):
            pool.wait_ge(row_out[m], 32 * (TT // 4))

    return scatter_sync, scatter_scalar, scatter_vector, scatter_gpsimd


def ffn_experts(nc, name, src, w, c, rt):
    w1a_t, w1b, w2a_t, w2b = w
    n_stage = 4
    with Stage(nc) as ctx:
        w1a_hl = ctx.enter_context(nc.sbuf_tensor(f"{name}_w1a", [P, KT, E, 2 * RANK], F32R))
        w1b_h = ctx.enter_context(nc.sbuf_tensor(f"{name}_w1bh", [P, E, FF], F32R))
        w1b_l = ctx.enter_context(nc.sbuf_tensor(f"{name}_w1bl", [P, E, FF], F32R))
        w2a_hl = ctx.enter_context(nc.sbuf_tensor(f"{name}_w2a", [P, FT, E, 2 * RANK], F32R))
        w2b_h = ctx.enter_context(nc.sbuf_tensor(f"{name}_w2bh", [P, E, D], F32R))
        w2b_l = ctx.enter_context(nc.sbuf_tensor(f"{name}_w2bl", [P, E, D], F32R))
        raw = ctx.enter_context(nc.sbuf_tensor(f"{name}_raw", [P, n_stage, FF], F32))
        cur_1a = ctx.enter_context(nc.sbuf_tensor(f"{name}_cur1a", [P, 2, KT, 2 * RANK], F32R))
        cur_2a = ctx.enter_context(nc.sbuf_tensor(f"{name}_cur2a", [P, 2, FT, 2 * RANK], F32R))
        cur_2b = ctx.enter_context(nc.sbuf_tensor(f"{name}_cur2b", [P, 2, 2, D], F32R))
        xs = ctx.enter_context(nc.sbuf_tensor(f"{name}_xs", [P, 2, D], F32))
        xh = ctx.enter_context(nc.sbuf_tensor(f"{name}_xh", [P, KT, P], F32R))
        xl = ctx.enter_context(nc.sbuf_tensor(f"{name}_xl", [P, KT, P], F32R))
        part = ctx.enter_context(nc.sbuf_tensor(f"{name}_part", [P, 2, RANK], F32))
        h1 = ctx.enter_context(nc.sbuf_tensor(f"{name}_h1", [P, 2, RANK], F32))
        h1_stack = ctx.enter_context(nc.sbuf_tensor(f"{name}_h1s", [P, 2, P], F32R))
        hg = ctx.enter_context(nc.sbuf_tensor(f"{name}_hg", [P, FF], F32))
        h_hl = ctx.enter_context(nc.sbuf_tensor(f"{name}_h_hl", [P, FT, 2, P], F32R))
        hh, hl = h_hl[:, :, 0], h_hl[:, :, 1]
        y1 = ctx.enter_context(nc.sbuf_tensor(f"{name}_y1", [P, P], F32))
        y1_add = ctx.enter_context(nc.sbuf_tensor(f"{name}_y1a", [P, P], F32))
        y1_h = ctx.enter_context(nc.sbuf_tensor(f"{name}_y1h", [P, P], F32R))
        y1_l = ctx.enter_context(nc.sbuf_tensor(f"{name}_y1l", [P, P], F32R))
        ys = ctx.enter_context(nc.sbuf_tensor(f"{name}_ys", [P, 2, D], F32))
        ps_x = ctx.enter_context(nc.psum_tensor(f"{name}_psx", [P, KT, P], F32))
        ps_a = ctx.enter_context(nc.psum_tensor(f"{name}_psa", [P, 512], F32))
        ps_b = ctx.enter_context(nc.psum_tensor(f"{name}_psb", [P, 2, 512], F32))
        ps_h = ctx.enter_context(nc.psum_tensor(f"{name}_psh", [P, FT, P], F32))
        ps_c = ctx.enter_context(nc.psum_tensor(f"{name}_psc", [P, 512], F32))
        ps_d = ctx.enter_context(nc.psum_tensor(f"{name}_psd", [P, 512], F32))
        ps_h1t = ps_a[:, 2 * RANK:2 * RANK + P]

        jobs = []
        for k in range(KT):
            v = w1a_t[k * P:(k + 1) * P, :]
            jobs.append((v, E * RANK, None, w1a_hl[:, k, :, 0:RANK], w1a_hl[:, k, :, RANK:2 * RANK], RANK))
        for f in range(FT):
            v = w2a_t[f * P:(f + 1) * P, :]
            jobs.append((v, E * RANK, None, w2a_hl[:, f, :, 0:RANK], w2a_hl[:, f, :, RANK:2 * RANK], RANK))
        for e in range(E):
            jobs.append((w1b[e * RANK:(e + 1) * RANK, :], FF, "twice", w1b_h[:, e], w1b_l[:, e], None))
        for e in range(0, E, 4):
            v = w2b[e * RANK:(e + 4) * RANK, :].rearrange("(e r) d -> r e d", r=RANK)
            jobs.append((v, 4 * D, "twice4", w2b_h[:, e:e + 4], w2b_l[:, e:e + 4], D))
        with Stage(nc) as ctx:
            scatter_sync, scatter_scalar, scatter_vector, scatter_gpsimd = scatter_programs(nc, ctx, name, src, c, rt)
            raw0 = ctx.semaphore(f"{name}_raw0")
            raw1 = ctx.semaphore(f"{name}_raw1")
            raw2 = ctx.semaphore(f"{name}_raw2")
            raw3 = ctx.semaphore(f"{name}_raw3")
            high_ready = ctx.semaphore(f"{name}_high")
            low_ready = ctx.semaphore(f"{name}_low")
            block = ctx.enter_context(nc.Block())
            raw_in = [raw0, raw1, raw2, raw3]
            need = [[] for _ in jobs]
            so_far = [0] * n_stage
            for n, job in enumerate(jobs):
                so_far[n % n_stage] += 32 if job[2] else 16
                need[n] = so_far[n % n_stage]

            def shaped(ap, width):
                return ap if width is None else ap.rearrange("p (e r) -> p e r", r=width)

            def load_raw(sp, n):
                v, size, kind, _h, _l, width = jobs[n]
                if n >= n_stage:
                    sp.wait_ge(low_ready, n - n_stage + 1)
                if kind is None:
                    sp.dma_start(raw[:, n % n_stage, 0:size], v).then_inc(raw_in[n % n_stage], 16)
                else:
                    for r in range(2):
                        dst = raw[r * RANK:(r + 1) * RANK, n % n_stage, 0:size]
                        if kind == "twice4":
                            dst = dst.rearrange("p (e d) -> p e d", d=D)
                        sp.dma_start(dst, v).then_inc(raw_in[n % n_stage], 16)

            @block.sync
            def _(sp):
                for i in range(n_stage):
                    scatter_sync(sp, i)
                for n in range(len(jobs)):
                    load_raw(sp, n)
                    if n_stage <= n < TT:
                        scatter_sync(sp, n)

            @block.scalar
            def _(act):
                for n, (_v, size, _k, high, _l, width) in enumerate(jobs):
                    if n < TT:
                        scatter_scalar(act, n)
                    act.wait_ge(raw_in[n % n_stage], need[n])
                    act.activation(high, shaped(raw[:, n % n_stage, 0:size], width), ACT.Copy).then_inc(high_ready, 1)

            @block.vector
            def _(dve):
                def split_low(n):
                    _v, size, _k, high, low, width = jobs[n]
                    dve.wait_ge(high_ready, n + 1)
                    dve.wait_ge(raw_in[n % n_stage], need[n])
                    dve.tensor_tensor(low, shaped(raw[:, n % n_stage, 0:size], width), high.bitcast(F32),
                                      ALU.subtract).then_inc(low_ready, 1)

                scatter_vector(dve, split_low)
                for n in range(TT, len(jobs)):
                    split_low(n)

            @block.gpsimd
            def _(pool):
                scatter_gpsimd(pool)

        names = ["xs0", "xs1", "xt", "xh", "xl", "a", "ap", "h1", "h1t", "h1h", "h1s", "b", "g0", "g1", "ht0", "ht1",
                 "hh0", "hh1", "hl0", "hl1", "c", "cp", "y1", "y1h", "y1s", "d", "ys", "st0", "st1",
                 "w1a", "w2a", "w2b"]
        with Stage(nc) as ctx:
            s = {n: ctx.semaphore(f"{name}_s_" + n) for n in names}
            block = ctx.enter_context(nc.Block())
            xs_tiles = rt["xs"][0:SLOTS, :].rearrange("(t p) d -> p t d", p=P)
            ys_tiles = rt["ys"].rearrange("(t p) d -> p t d", p=P)

            def expert(eng, t):
                return eng.value_load(rt["tile_expert"][0:1, bass.ds(t.j, 1)], min_val=0, max_val=E - 1)

            @block.gpsimd
            def _(pool):
                sk = Skew(pool, SLOT_TILES)

                def take_1a(t):
                    e = expert(pool, t)
                    at_least(pool, s["a"], t.j - 1)
                    pool.tensor_copy(cur_1a[:, t.p].unsqueeze(2), w1a_hl[:, :, bass.ds(e, 1), :]).then_inc(s["w1a"], 1)

                def take_2b(t):
                    e = expert(pool, t)
                    at_least(pool, s["d"], t.j - 1)
                    pool.tensor_copy(cur_2b[:, t.p, 0:1], w2b_h[:, bass.ds(e, 1), :])
                    pool.tensor_copy(cur_2b[:, t.p, 1:2], w2b_l[:, bass.ds(e, 1), :]).then_inc(s["w2b"], 1)

                def iteration(t):
                    sk.do(take_1a, t.plus(3))
                    sk.do(take_2b, t.plus(-1))

                sk.run(iteration, -3, PEELED, SLOT_TILES + 2)

            @block.sync
            def _(sp):
                def load(t):
                    at_least(sp, s["xt"], t.j - 1)
                    sp.dma_start(xs[:, t.p:t.p + 1], xs_tiles[:, bass.ds(t.j, 1), :]).then_inc(s[f"xs{t.p}"], 16)

                def store(t):
                    sp.wait_ge(s["ys"], t.j + 1)
                    sp.dma_start(ys_tiles[:, bass.ds(t.j, 1), :], ys[:, t.p:t.p + 1]).then_inc(s[f"st{t.p}"], 16)

                def iteration(t):
                    sk.do(load, t.plus(4))
                    sk.do(store, t.plus(-2))

                sk = Skew(sp, SLOT_TILES)
                sk.run(iteration, -4, PEELED, SLOT_TILES + 2)
                for p in range(2):
                    sp.wait_ge(s[f"st{p}"], 16 * (SLOT_TILES // 2))

            @block.tensor
            def _(pe):
                sk = Skew(pe, SLOT_TILES)
                ident = c["ident"][:]

                def transpose_x(t):
                    pe.wait_ge(s[f"xs{t.p}"], (t.half + 1) * 16)
                    at_least(pe, s["xl"], t.j)
                    for k in range(KT):
                        last = pe.transpose(ps_x[:, k], xs[:, t.p, k * P:(k + 1) * P], ident)
                    last.then_inc(s["xt"], 1)

                def first_down(t):
                    pe.wait_ge(s["xh"], t.j + 1)
                    pe.wait_ge(s["xl"], t.j + 1)
                    at_least(pe, s["h1s"], t.j)
                    at_least(pe, s["h1"], t.j)
                    pe.wait_ge(s["w1a"], t.j + 1)
                    for k in range(KT):
                        pe.matmul(ps_a[:, 0:2 * RANK], xh[:, k], cur_1a[:, t.p, k],
                                  start=(k == 0), stop=False, skip_group_check=True)
                    for k in range(KT):
                        last = pe.matmul(ps_a[:, 0:RANK], xl[:, k],
                                         cur_1a[:, t.p, k, 0:RANK],
                                         start=False, stop=(k == KT - 1), skip_group_check=True)
                    last.then_inc(s["a"], 1)

                def transpose_h1(t):
                    pe.wait_ge(s["h1"], t.j + 1)
                    pe.transpose(ps_h1t, h1[:].rearrange("p a r -> p (a r)"), ident).then_inc(s["h1t"], 1)

                def first_up(t, e):
                    pe.wait_ge(s["h1s"], t.j + 1)
                    for n in range(2):
                        at_least(pe, s[f"g{n}"], t.j)
                        for m, wt in enumerate((w1b_h, w1b_l)):
                            last = pe.matmul(ps_b[:, n], h1_stack[:, t.p],
                                             wt[:, bass.ds(e, 1), n * 512:(n + 1) * 512].rearrange("p a f -> p (a f)"),
                                             start=(m == 0), stop=(m == 1))
                        last.then_inc(s["b"], 1)

                def transpose_h(t, n):
                    pe.wait_ge(s[f"g{n}"], t.j + 1)
                    at_least(pe, s[f"hl{n}"], t.j)
                    for f in range(4 * n, 4 * n + 4):
                        last = pe.transpose(ps_h[:, f], hg[:, f * P:(f + 1) * P], ident)
                    last.then_inc(s[f"ht{n}"], 1)

                def second_down(t):
                    at_least(pe, s["y1"], t.j)
                    pe.wait_ge(s["w2a"], t.j + 1)
                    for n in range(2):
                        pe.wait_ge(s[f"hh{n}"], t.j + 1)
                        pe.wait_ge(s[f"hl{n}"], t.j + 1)
                        for f in range(4 * n, 4 * n + 4):
                            last = pe.matmul(ps_c[:, 0:2 * P], cur_2a[:, t.p, f], h_hl[:, f].rearrange("p a n -> p (a n)"),
                                             start=(f == 0), stop=(f == FT - 1))
                    last.then_inc(s["c"], 1)

                def second_up(t):
                    pe.wait_ge(s["y1s"], t.j + 1)
                    pe.wait_ge(s["w2b"], t.j + 1)
                    at_least(pe, s["ys"], t.j)
                    for m, (part_y, part_w) in enumerate(((y1_h, 0), (y1_h, 1), (y1_l, 0))):
                        last = pe.matmul(ps_d[:, 0:D], part_y[:], cur_2b[:, t.p, part_w], start=(m == 0), stop=(m == 2))
                    last.then_inc(s["d"], 1)

                def iteration(t):
                    sk.do(lambda u: first_up(u, expert(pe, u)), t)
                    sk.do(second_down, t.plus(-1))
                    sk.do(second_up, t.plus(-2))
                    sk.do(first_down, t.plus(2))
                    sk.do(lambda u: transpose_h(u, 0), t)
                    sk.do(transpose_h1, t.plus(2))
                    sk.do(lambda u: transpose_h(u, 1), t)
                    sk.do(transpose_x, t.plus(3))

                sk.run(iteration, -3, PEELED, SLOT_TILES + 2)

            @block.scalar
            def _(act):
                sk = Skew(act, SLOT_TILES)
                def x_high(t):
                    act.wait_ge(s["xt"], t.j + 1)
                    at_least(act, s["a"], t.j)
                    act.activation(xh[:], ps_x[:], ACT.Copy).then_inc(s["xh"], 1)

                def h1_part(t):
                    act.wait_ge(s["a"], t.j + 1)
                    at_least(act, s["h1"], t.j)
                    act.activation(part[:, 0], ps_a[:, RANK:2 * RANK], ACT.Copy).then_inc(s["ap"], 1)

                def h1_high(t):
                    act.wait_ge(s["h1t"], t.j + 1)
                    at_least(act, s["b"], (t.j - 1) * 2)
                    act.activation(h1_stack[:, t.p], ps_h1t, ACT.Copy).then_inc(s["h1h"], 1)

                def gelu(t, n):
                    act.wait_ge(s["b"], t.j * 2 + n + 1)
                    at_least(act, s[f"ht{n}"], t.j)
                    act.activation(hg[:, n * 512:(n + 1) * 512], ps_b[:, n], ACT.Gelu).then_inc(s[f"g{n}"], 1)

                def h_high(t, n):
                    act.wait_ge(s[f"ht{n}"], t.j + 1)
                    at_least(act, s["c"], t.j)
                    act.activation(hh[:, 4 * n:4 * n + 4], ps_h[:, 4 * n:4 * n + 4], ACT.Copy).then_inc(s[f"hh{n}"], 1)

                def y1_part(t):
                    act.wait_ge(s["c"], t.j + 1)
                    at_least(act, s["y1"], t.j)
                    act.activation(y1_add[:], ps_c[:, P:2 * P], ACT.Copy).then_inc(s["cp"], 1)

                def y1_high(t):
                    act.wait_ge(s["y1"], t.j + 1)
                    at_least(act, s["d"], t.j)
                    act.activation(y1_h[:], y1[:], ACT.Copy).then_inc(s["y1h"], 1)

                def y_out(t):
                    act.wait_ge(s["d"], t.j + 1)
                    at_least(act, s[f"st{t.p}"], t.half * 16)
                    act.activation(ys[:, t.p], ps_d[:, 0:D], ACT.Copy).then_inc(s["ys"], 1)

                def iteration(t):
                    sk.do(lambda u: gelu(u, 0), t)
                    sk.do(lambda u: gelu(u, 1), t)
                    sk.do(h1_part, t.plus(2))
                    sk.do(y1_part, t.plus(-1))
                    sk.do(lambda u: h_high(u, 0), t)
                    sk.do(h1_high, t.plus(2))
                    sk.do(lambda u: h_high(u, 1), t)
                    sk.do(y1_high, t.plus(-1))
                    sk.do(y_out, t.plus(-2))
                    sk.do(x_high, t.plus(3))

                sk.run(iteration, -3, PEELED, SLOT_TILES + 2)

            @block.vector
            def _(dve):
                sk = Skew(dve, SLOT_TILES)
                def take_2a(t):
                    e = expert(dve, t)
                    at_least(dve, s["c"], t.j - 1)
                    dve.tensor_copy(cur_2a[:, t.p].unsqueeze(2), w2a_hl[:, :, bass.ds(e, 1), :]).then_inc(s["w2a"], 1)

                def x_low(t):
                    dve.wait_ge(s["xh"], t.j + 1)
                    at_least(dve, s["a"], t.j)
                    dve.tensor_tensor(xl[:], ps_x[:], xh[:].bitcast(F32), ALU.subtract).then_inc(s["xl"], 1)

                def h1_sum(t):
                    dve.wait_ge(s["ap"], t.j + 1)
                    at_least(dve, s["h1t"], t.j)
                    dve.tensor_tensor(h1[:], ps_a[:, 0:RANK].unsqueeze(1).broadcast_to([P, 2, RANK]),
                                      part[:, 0].unsqueeze(1).broadcast_to([P, 2, RANK]), ALU.add).then_inc(s["h1"], 1)

                def h1_low(t):
                    dve.wait_ge(s["h1h"], t.j + 1)
                    low = h1_stack[RANK:P, t.p]
                    dve.tensor_tensor(low, ps_h1t[RANK:P], low.bitcast(F32), ALU.subtract).then_inc(s["h1s"], 1)

                def h_low(t, n):
                    dve.wait_ge(s[f"hh{n}"], t.j + 1)
                    at_least(dve, s["c"], t.j)
                    dve.tensor_tensor(hl[:, 4 * n:4 * n + 4], ps_h[:, 4 * n:4 * n + 4],
                                      hh[:, 4 * n:4 * n + 4].bitcast(F32), ALU.subtract).then_inc(s[f"hl{n}"], 1)

                def y1_sum(t):
                    dve.wait_ge(s["cp"], t.j + 1)
                    at_least(dve, s["y1h"], t.j)
                    at_least(dve, s["y1s"], t.j)
                    dve.tensor_tensor(y1[:], ps_c[:, 0:P], y1_add[:], ALU.add).then_inc(s["y1"], 1)

                def y1_low(t):
                    dve.wait_ge(s["y1h"], t.j + 1)
                    at_least(dve, s["d"], t.j)
                    dve.tensor_tensor(y1_l[:], y1[:], y1_h[:].bitcast(F32), ALU.subtract).then_inc(s["y1s"], 1)

                def iteration(t):
                    sk.do(take_2a, t)
                    sk.do(h1_sum, t.plus(2))
                    sk.do(y1_sum, t.plus(-1))
                    sk.do(lambda u: h_low(u, 0), t)
                    sk.do(h1_low, t.plus(2))
                    sk.do(lambda u: h_low(u, 1), t)
                    sk.do(y1_low, t.plus(-1))
                    sk.do(x_low, t.plus(3))

                sk.run(iteration, -3, PEELED, SLOT_TILES + 2)


def ffn_combine(nc, name, src, dst, c, rt):
    nb = 4
    with Stage(nc) as ctx:
        xt = ctx.enter_context(nc.sbuf_tensor(f"{name}_x", [P, nb, D], F32))
        y = ctx.enter_context(nc.sbuf_tensor(f"{name}_y", [P, nb, TOPK, D], F32))
        x_in = [ctx.semaphore(f"{name}_xin{m}") for m in range(nb)]
        y_in = [ctx.semaphore(f"{name}_yin{m}") for m in range(nb)]
        added = ctx.semaphore(f"{name}_added")
        summed = ctx.semaphore(f"{name}_summed")
        stored = [ctx.semaphore(f"{name}_stored{m}") for m in range(nb)]
        block = ctx.enter_context(nc.Block())
        src_t, dst_t = ffn_rows(src), ffn_rows(dst)

        @block.sync
        def _(sp):
            for i in range(TT):
                if i >= nb:
                    sp.wait_ge(stored[i % nb], 16 * (i // nb))
                sp.dma_start(xt[:, i % nb], src_t[i]).then_inc(x_in[i % nb], 16)

        @block.gpsimd
        def _(pool):
            for i in range(TT):
                if i >= nb:
                    pool.wait_ge(summed, i - nb + 1)
                for k in range(TOPK):
                    col = i * TOPK + k
                    pool.indirect_dma_start(
                        y[:, i % nb, k], None, rt["ys"],
                        bass.IndirectOffsetOnAxis(ap=rt["pos_gather"][:, col:col + 1], axis=0)).then_inc(y_in[i % nb], 16)

        @block.vector
        def _(dve):
            for i in range(TT):
                m = i % nb
                dve.wait_ge(x_in[m], 16 * (i // nb + 1))
                dve.wait_ge(y_in[m], 32 * (i // nb + 1))
                dve.scalar_tensor_tensor(xt[:, m], y[:, m, 0], rt["half_w"][:, i * TOPK:i * TOPK + 1], xt[:, m],
                                         ALU.mult, ALU.add).then_inc(added, 1)
                dve.wait_ge(added, i + 1)
                dve.scalar_tensor_tensor(xt[:, m], y[:, m, 1], rt["half_w"][:, i * TOPK + 1:i * TOPK + 2], xt[:, m],
                                         ALU.mult, ALU.add).then_inc(summed, 1)

        @block.scalar
        def _(act):
            for i in range(TT):
                act.wait_ge(summed, i + 1)
                act.dma_start(dst_t[i], xt[:, i % nb]).then_inc(stored[i % nb], 16)
            for m in range(nb):
                act.wait_ge(stored[m], 16 * (TT // nb))


H = 16
HD = D // H
B = BATCHES
S_LEN = SEQ
C = 16
TILES = S_LEN // C
QUAD = 32
NQ = P // QUAD
HPQ = H // NQ
GROUP = P // B
GROUPS = TILES // GROUP
PROJ = 4 * D + 2 * H
THIRDS = 3
THIRD = PROJ // THIRDS
HALF = P // HD
L2_EPS = 1e-12
INV_COLS = H * C + 4 * H
ATT_COLS = H * C + H
SC_COLS = 4 * H


def tile_rows(t):
    return bass.ds(t.j, 1)


def project(nc, x, w, c, d):
    with Stage(nc) as ctx:
        def sb(name, shape, dt=F32):
            return ctx.enter_context(nc.sbuf_tensor("a_" + name, shape, dt))

        def pb(name, shape):
            return ctx.enter_context(nc.psum_tensor("a_" + name, shape, F32))

        raw = sb("raw", [P, KT, PROJ])
        w_h, w_l = sb("w_h", [P, KT, PROJ], F32R), sb("w_l", [P, KT, PROJ], F32R)
        xt, xn = sb("xt", [P, 2, D]), sb("xn", [P, 2, D])
        st, mv = sb("st", [P, 2, 6]), sb("mv", [P, 2, 2])
        sd, rs = sb("sd", [P, 2]), sb("rs", [P, 2])
        x_h, x_l = sb("x_h", [P, KT, P], F32R), sb("x_l", [P, KT, P], F32R)
        sq, mark = sb("sq", [P, 2 * D]), sb("mark", [P, 1])
        ss, nrm, rn = sb("ss", [P, 2 * H]), sb("nrm", [P, 2 * H]), sb("rn", [P, 2, 2 * H])
        proj = sb("proj", [P, 2, PROJ])
        tok = sb("tok", [P, 2, 2 * D])
        kqt = sb("kqt", [P, 2, 2 * B, 2, C])
        kbd = sb("kbd", [P, 2, 2, HALF, P])
        gram = sb("gram", [P, 2, 2 * D])
        ps_x, ps_p = pb("ps_x", [P, 512]), pb("ps_p", [P, THIRDS, 512])
        ps_t, ps_g = pb("ps_t", [P, 2, 2, P]), pb("ps_g", [P, 2, 512])

        wraw, wh, wl = (ctx.semaphore("a_" + n) for n in ("wraw", "wh", "wl"))
        with nc.Block() as block:
            @block.sync
            def _(sp):
                col = 0
                for a in w:
                    n = a.shape[1]
                    sp.dma_start(raw[:, :, col:col + n], a.rearrange("(k p) n -> p k n", p=P)).then_inc(wraw, 16)
                    col += n

            @block.scalar
            def _(act):
                act.wait_ge(wraw, 16 * len(w))
                act.activation(w_h[:], raw[:], ACT.Copy).then_inc(wh, 1)

            @block.vector
            def _(dve):
                dve.wait_ge(wraw, 16 * len(w))
                dve.wait_ge(wh, 1)
                dve.tensor_tensor(w_l[:], raw[:], w_h[:].bitcast(F32), ALU.subtract).then_inc(wl, 1)
                dve.wait_ge(wl, 1)

        names = ["p0", "p1", "p2", "c0", "c1", "c2", "vg0", "vg1", "x0", "x1", "mv", "sd", "rs", "cl", "chain", "xn", "xt", "xh", "xl", "sq", "ss", "nrm", "rn", "unit",
                 "tqk", "kqt", "kbd0", "kbd1", "g", "gev", "tok0", "tok1", "ab0", "ab1", "gst0", "gst1"]
        s = {n: ctx.semaphore("a_" + n) for n in names}
        x_t = x.rearrange("(c p) d -> p c d", p=P)
        tok_t = d["tok"].rearrange("(c p) n -> p c n", p=P)
        ab_t = d["ab"].rearrange("(c b t) n -> c t b n", b=B, t=C)
        gram_t = d["gram"].rearrange("c (bh r) f -> c r bh f", bh=2)
        block = ctx.enter_context(nc.Block())

        @block.sync
        def _(sp):
            sk = Skew(sp, TILES)

            def load(t):
                at_least(sp, s["xn"], t.j - 1)
                sp.dma_start(xt[:, t.p:t.p + 1], x_t[:, tile_rows(t)]).then_inc(s[f"x{t.p}"], 16)

            def store(t):
                sp.wait_ge(s["c1"], t.j + 1)
                sp.wait_ge(s["c2"], t.j + 1)
                sp.dma_start(tok_t[:, tile_rows(t), 2 * D:4 * D], proj[:, t.p:t.p + 1, 2 * D:4 * D]
                             ).then_inc(s[f"vg{t.p}"], 16)
                sp.wait_ge(s["unit"], t.j + 1)
                sp.dma_start(ab_t[tile_rows(t)].rearrange("c t b n -> (c t) b n"), proj[:, t.p, 4 * D:PROJ]
                             ).then_inc(s[f"ab{t.p}"], 16)
                sp.dma_start(tok_t[:, tile_rows(t), 0:2 * D], tok[:, t.p:t.p + 1]).then_inc(s[f"tok{t.p}"], 16)

            def store_gram(t):
                sp.wait_ge(s["gev"], t.j + 1)
                sp.dma_start(gram_t[tile_rows(t)].rearrange("a r bh f -> r (a bh) f"),
                             gram[:, t.p].rearrange("p (bh f) -> p bh f", bh=2)).then_inc(s[f"gst{t.p}"], 16)

            def iteration(t):
                sk.do(load, t.plus(3))
                sk.do(store, t.plus(-1))
                sk.do(store_gram, t.plus(-3))

            sk.run(iteration, -3, 6, TILES + 3)
            for p in range(2):
                for n in ("tok", "vg", "ab", "gst"):
                    sp.wait_ge(s[f"{n}{p}"], 16 * (TILES // 2))

        @block.tensor
        def _(pe):
            sk = Skew(pe, TILES)

            def transpose_x(t):
                pe.wait_ge(s["xn"], t.j + 1)
                at_least(pe, s["xl"], t.j)
                for k in range(KT):
                    last = pe.transpose(ps_x[:, k * P:(k + 1) * P], xn[:, t.p, k * P:(k + 1) * P], c["ident"][:])
                last.then_inc(s["xt"], 1)

            def products(t):
                pe.wait_ge(s["xh"], t.j + 1)
                pe.wait_ge(s["xl"], t.j + 1)
                for n in range(THIRDS):
                    at_least(pe, s[f"c{n}"], t.j)
                    m = 0
                    for xx, ww in ((x_h, w_h), (x_h, w_l), (x_l, w_h)):
                        for k in range(KT):
                            last = pe.matmul(ps_p[:, n, 0:THIRD], xx[:, k], ww[:, k, n * THIRD:(n + 1) * THIRD],
                                             start=(m == 0), stop=(m == 5))
                            m += 1
                    last.then_inc(s[f"p{n}"], 1)

            def transpose_qk(t):
                pe.wait_ge(s["unit"], t.j + 1)
                at_least(pe, s["kqt"], t.j)
                for n in range(2):
                    for half in range(2):
                        col = (1 - n) * D + half * P
                        last = pe.transpose(ps_t[:, n, half], tok[:, t.p, col:col + P], c["ident"][:])
                last.then_inc(s["tqk"], 1)

            def chunk_products(t):
                pe.wait_ge(s["kqt"], t.j + 1)
                pe.wait_ge(s["kbd0"], t.j + 1)
                pe.wait_ge(s["kbd1"], t.j + 1)
                at_least(pe, s["gev"], t.j - 1)
                for b in range(B):
                    q, bh = b % NQ, b // NQ
                    for half in range(2):
                        last = pe.matmul(ps_g[q * QUAD:(q + 1) * QUAD, t.p, (2 * bh + half) * P:(2 * bh + half + 1) * P],
                                         kqt[:, t.p, half * B + b].rearrange("p n t -> p (n t)"),
                                         kbd[:, t.p, half, :, b * C:(b + 1) * C], start=True, stop=True)
                last.then_inc(s["g"], 1)

            def iteration(t):
                sk.do(products, t)
                sk.do(transpose_x, t.plus(1))
                sk.do(chunk_products, t.plus(-3))
                sk.do(transpose_qk, t.plus(-2))

            sk.run(iteration, -2, 6, TILES + 3)

        @block.scalar
        def _(act):
            sk = Skew(act, TILES)

            def std(t):
                act.wait_ge(s["mv"], t.j + 1)
                at_least(act, s["chain"], t.j - 1)
                act.activation(sd[:, t.p:t.p + 1], mv[:, t.p, 1:2], ACT.Sqrt, bias=c["eps"][:, 0:1]).then_inc(s["sd"], 1)

            def norms(t):
                act.wait_ge(s["ss"], t.j + 1)
                at_least(act, s["rn"], t.j)
                act.activation(nrm[:], ss[:], ACT.Sqrt).then_inc(s["nrm"], 1)

            def squares(t):
                act.wait_ge(s["c0"], t.j + 1)
                act.wait_ge(s["c1"], t.j + 1)
                at_least(act, s["ss"], t.j)
                act.activation(sq[:], proj[:, t.p, 0:2 * D], ACT.Square).then_inc(s["sq"], 1)

            def x_high(t):
                act.wait_ge(s["xt"], t.j + 1)
                at_least(act, s["p2"], t.j)
                act.activation(x_h[:], ps_x[:, 0:KT * P], ACT.Copy).then_inc(s["xh"], 1)

            def copy_third(t, n):
                act.wait_ge(s[f"p{n}"], t.j + 1)
                if n < 2:
                    at_least(act, s["unit"], t.j - 1)
                if n > 0:
                    at_least(act, s[f"vg{t.p}"], t.half * 16)
                if n == 2:
                    at_least(act, s[f"ab{t.p}"], t.half * 16)
                act.activation(proj[:, t.p, n * THIRD:(n + 1) * THIRD], ps_p[:, n, 0:THIRD], ACT.Copy
                               ).then_inc(s[f"c{n}"], 1)

            def copy_kq(t):
                act.wait_ge(s["tqk"], t.j + 1)
                at_least(act, s["g"], t.j - 1)
                at_least(act, s["kbd0"], t.j - 1)
                at_least(act, s["kbd1"], t.j - 1)
                for half in range(2):
                    last = act.activation(kqt[:, t.p, half * B:(half + 1) * B],
                                          ps_t[:, :, half].rearrange("p n (t b) -> p b n t", b=B), ACT.Copy)
                last.then_inc(s["kqt"], 1)

            def copy_gram(t):
                act.wait_ge(s["g"], t.j + 1)
                at_least(act, s[f"gst{t.p}"], t.half * 16)
                act.activation(gram[:, t.p], ps_g[:, t.p], ACT.Copy).then_inc(s["gev"], 1)

            def iteration(t):
                sk.do(norms, t.plus(-1))
                sk.do(std, t.plus(2))
                sk.do(lambda u: copy_third(u, 0), t)
                sk.do(lambda u: copy_third(u, 1), t)
                sk.do(x_high, t.plus(1))
                sk.do(lambda u: copy_third(u, 2), t)
                sk.do(squares, t)
                sk.do(copy_gram, t.plus(-3))
                sk.do(copy_kq, t.plus(-2))

            sk.run(iteration, -2, 6, TILES + 3)

        @block.vector
        def _(dve):
            sk = Skew(dve, TILES)

            def moments(t):
                dve.wait_ge(s[f"x{t.p}"], (t.half + 1) * 16)
                at_least(dve, s["mv"], t.j - 1)
                at_least(dve, s["xn"], t.j - 1)
                dve.bn_stats(st[:, t.p], xt[:, t.p]).then_inc(s["chain"], 1)
                dve.wait_ge(s["chain"], t.j + 1)
                dve.tensor_copy(mark[:], st[:, t.p, 0:1])
                dve.bn_aggr(mv[:, t.p], st[:, t.p]).then_inc(s["mv"], 1)

            def normalise(t):
                dve.wait_ge(s["sd"], t.j + 1)
                dve.reciprocal(rs[:, t.p:t.p + 1], sd[:, t.p:t.p + 1]).then_inc(s["rs"], 1)
                dve.wait_ge(s["rs"], t.j + 1)
                at_least(dve, s["xt"], t.j - 1)
                dve.tensor_scalar(xn[:, t.p], xt[:, t.p], mv[:, t.p, 0:1], rs[:, t.p:t.p + 1],
                                  ALU.subtract, ALU.mult).then_inc(s["xn"], 1)

            def sums(t):
                dve.wait_ge(s["sq"], t.j + 1)
                at_least(dve, s["nrm"], t.j)
                dve.tensor_reduce(ss[:], sq[:].rearrange("p (h e) -> p h e", e=HD), AX.X, ALU.add).then_inc(s["ss"], 1)

            def unit(t):
                dve.wait_ge(s["nrm"], t.j + 1)
                at_least(dve, s["rn"], t.j)
                dve.tensor_scalar(rn[:, 0], nrm[:], L2_EPS, None, ALU.max).then_inc(s["cl"], 1)
                dve.wait_ge(s["cl"], t.j + 1)
                at_least(dve, s["unit"], t.j)
                dve.reciprocal(rn[:, 1], rn[:, 0]).then_inc(s["rn"], 1)
                dve.wait_ge(s["rn"], t.j + 1)
                at_least(dve, s[f"tok{t.p}"], t.half * 16)
                at_least(dve, s["tqk"], t.j - 1)
                for n in range(2):
                    last = dve.tensor_tensor(tok[:, t.p, (1 - n) * D:(2 - n) * D].rearrange("p (h e) -> p h e", e=HD),
                                             proj[:, t.p, n * D:(n + 1) * D].rearrange("p (h e) -> p h e", e=HD),
                                             rn[:, 1, n * H:(n + 1) * H].unsqueeze(2).broadcast_to([P, H, HD]), ALU.mult)
                last.then_inc(s["unit"], 1)

            def x_low(t):
                dve.wait_ge(s["xh"], t.j + 1)
                at_least(dve, s["p2"], t.j)
                dve.tensor_tensor(x_l[:].rearrange("p k n -> p (k n)"), ps_x[:, 0:KT * P],
                                  x_h[:].bitcast(F32).rearrange("p k n -> p (k n)"), ALU.subtract).then_inc(s["xl"], 1)

            def spread0(t):
                dve.wait_ge(s["kqt"], t.j + 1)
                at_least(dve, s["g"], t.j - 1)
                dve.tensor_tensor(kbd[:, t.p, 0].rearrange("p h (b t) -> p h b t", b=B),
                                  kqt[:, t.p, 0:B, 0].unsqueeze(1).broadcast_to([P, HALF, B, C]),
                                  c["mask16"][:].unsqueeze(2).unsqueeze(3).broadcast_to([P, HALF, B, C]), ALU.mult).then_inc(s["kbd0"], 1)

            def iteration(t):
                sk.do(sums, t.plus(-1))
                sk.do(moments, t.plus(2))
                sk.do(spread0, t.plus(-3))
                sk.do(normalise, t.plus(2))
                sk.do(x_low, t.plus(1))
                sk.do(unit, t.plus(-1))

            
            
            sk.run(iteration, -2, 6, TILES + 3)

        @block.gpsimd
        def _(pool):
            sk = Skew(pool, TILES)

            def spread1(t):
                pool.wait_ge(s["kqt"], t.j + 1)
                at_least(pool, s["g"], t.j - 1)
                pool.tensor_tensor(kbd[:, t.p, 1].rearrange("p h (b t) -> p h b t", b=B),
                                   kqt[:, t.p, B:2 * B, 0].unsqueeze(1).broadcast_to([P, HALF, B, C]),
                                   c["mask16"][:].unsqueeze(2).unsqueeze(3).broadcast_to([P, HALF, B, C]), ALU.mult).then_inc(s["kbd1"], 1)

            sk.run(lambda t: sk.do(spread1, t.plus(-2)), -1, 6, TILES + 3)


def solve_chunks(nc, bias, c, d):
    with Stage(nc) as ctx:
        def sb(name, shape, dt=F32):
            return ctx.enter_context(nc.sbuf_tensor("b_" + name, shape, dt))

        kk_qk = sb("kk_qk", [P, 2, 2, C, H, C])
        ab = sb("ab", [P, 2, C, 2 * H])
        ab_bias = sb("bias", [P, 2 * H])
        gates = sb("gates", [P, C, 2 * H])
        neg_b = sb("neg_b", [P, C, H])
        decay = sb("decay", [P, C, H, C])
        inv_scal2 = sb("inv", [P, 2, C, INV_COLS])
        att_g2 = sb("att", [P, 2, C, ATT_COLS])
        area = max(i * (C - 1 - i) for i in range(C))
        tmp = sb("tmp", [P, H * area])
        end_decay = sb("end_decay", [P, 2, H])
        loaded = [ctx.semaphore(f"b_in{m}") for m in range(2)]
        stored = [ctx.semaphore(f"b_stored{m}") for m in range(2)]
        names = ["bias", "init", "biased", "gates", "chain", "pchain", "ready", "pready"]
        s = {n: ctx.semaphore("b_" + n) for n in names}
        block = ctx.enter_context(nc.Block())
        HV = 12

        @block.sync
        def _(sp):
            sp.dma_start(ab_bias[:], bias.partition_broadcast(P)).then_inc(s["bias"], 16)
            for g in range(GROUPS):
                if g >= 2:
                    sp.wait_ge(s["ready"], g - 1)
                    sp.wait_ge(s["pready"], g - 1)
                rows = slice(g * P, (g + 1) * P)
                sp.dma_start(kk_qk[:, g % 2].rearrange("p a t h i -> p (a t h i)"),
                             d["gram"].rearrange("c (b r) f -> (c b) (r f)", b=B)[rows]).then_inc(loaded[g % 2], 16)
                sp.dma_start(ab[:, g % 2].rearrange("p t h -> p (t h)"),
                             d["ab"].rearrange("(c t) n -> c (t n)", t=C)[rows]).then_inc(loaded[g % 2], 16)

        @block.scalar
        def _(act):
            for g in range(GROUPS):
                act.wait_ge(s["biased"], g + 1)
                act.activation(gates[:], ab[:, g % 2], ACT.Sigmoid).then_inc(s["gates"], 1)
                act.wait_ge(s["ready"], g + 1)
                act.wait_ge(s["pready"], g + 1)
                rows = slice(g * P, (g + 1) * P)
                act.dma_start(d["inv"][rows], inv_scal2[:, g % 2].rearrange("p j n -> p (j n)")).then_inc(stored[g % 2], 16)
                act.dma_start(d["att"][rows], att_g2[:, g % 2].rearrange("p i n -> p (i n)")).then_inc(stored[g % 2], 16)
                act.dma_start(d["end"].rearrange("q c (b m) -> c b q m", b=B)[g * GROUP:(g + 1) * GROUP]
                              .rearrange("c b q m -> (c b) q m"),
                              end_decay[:, g % 2].rearrange("p (q m) -> p q m", q=NQ)).then_inc(stored[g % 2], 16)
            for m in range(2):
                act.wait_ge(stored[m], 48 * (GROUPS // 2))

        def heads(eng, sem, g, h0, h1, count):
            def then(ins):
                count[0] += 1
                ins.then_inc(s[sem], 1)
                eng.wait_ge(s[sem], count[0])

            n = h1 - h0
            hs = slice(h0, h1)
            inv_scal, att_g = inv_scal2[:, g % 2], att_g2[:, g % 2]
            inv = inv_scal[:, :, 0:H * C].rearrange("p j (h t) -> p j h t", h=H)
            att = att_g[:, :, 0:H * C].rearrange("p i (h t) -> p i h t", h=H)
            scal = inv_scal[:, :, H * C:INV_COLS]
            kk, qk = kk_qk[:, g % 2, 0, :, hs], kk_qk[:, g % 2, 1, :, hs]
            al, be = gates[:, :, h0:h1], gates[:, :, H + h0:H + h1]
            dec, iv, at, nb = decay[:, :, hs], inv[:, :, hs], att[:, :, hs], neg_b[:, :, hs]
            eng.wait_ge(s["gates"], g + 1)
            if g >= 2:
                eng.wait_ge(stored[g % 2], 48 * (g // 2))
            then(eng.tensor_scalar(nb, be, -1.0, None, ALU.mult))
            for t in range(1, C):
                then(eng.tensor_tensor(dec[:, t, :, 0:t], dec[:, t - 1, :, 0:t],
                                       al[:, t].unsqueeze(2).broadcast_to([P, n, t]), ALU.mult))
            for t in range(1, C):
                last = eng.tensor_tensor(kk[:, t], kk[:, t], dec[:, t - 1], ALU.mult)
            then(last)
            for t in range(1, C):
                last = eng.tensor_tensor(kk[:, t], kk[:, t], nb[:, t].unsqueeze(2).broadcast_to([P, n, C]), ALU.mult)
            then(last)
            for t in range(C):
                last = eng.tensor_tensor(at[:, :, :, t].rearrange("p i h -> p h i"), qk[:, t], dec[:, t], ALU.mult)
            sc = scal[:, :, h0:h1], scal[:, :, H + h0:H + h1], scal[:, :, 2 * H + h0:2 * H + h1], \
                scal[:, :, 3 * H + h0:3 * H + h1]
            then(eng.tensor_tensor(sc[1], dec[:, :, :, 0], al[:, 0:1].broadcast_to([P, C, n]), ALU.mult))
            eng.tensor_copy(sc[0][:, 0], nb[:, 0])
            eng.tensor_tensor(sc[0][:, 1:C], sc[1][:, 0:C - 1], nb[:, 1:C], ALU.mult)
            eng.tensor_copy(sc[2].rearrange("p t h -> p h t"), dec[:, C - 1])
            eng.tensor_copy(att_g[:, :, H * C + h0:H * C + h1], sc[1])
            eng.tensor_copy(end_decay[:, g % 2, hs], sc[1][:, C - 1])
            eng.tensor_copy(sc[3], be)
            for t in range(1, C):
                last = eng.tensor_copy(iv[:, :, :, t].rearrange("p j h -> p h j"), kk[:, t])
            then(last)
            then(eng.memset(iv_first(iv, n), 0.0))
            for t in range(C):
                last = eng.memset(iv[:, t, :, t], 1.0)
            then(last)
            for i in range(1, C - 1):
                nt = C - 1 - i
                part = tmp[:, h0 * area:h0 * area + n * i * nt].rearrange("p (j h t) -> p j h t", j=i, h=n)
                then(eng.tensor_tensor(part, kk[:, i + 1:C, :, i].rearrange("p t h -> p h t").unsqueeze(1)
                                       .broadcast_to([P, i, n, nt]),
                                       iv[:, 0:i, :, i].unsqueeze(3).broadcast_to([P, i, n, nt]), ALU.mult))
                then(eng.tensor_tensor(iv[:, 0:i, :, i + 1:C], iv[:, 0:i, :, i + 1:C], part, ALU.add))

        def iv_first(iv, n):
            return iv[:, 1:C, :, 0]

        @block.vector
        def _(dve):
            count = [0]
            dve.memset(decay[:], 0.0).then_inc(s["init"], 1)
            dve.wait_ge(s["init"], 1)
            for t in range(C):
                last = dve.memset(decay[:, t, :, t], 1.0)
            last.then_inc(s["init"], 1)
            dve.wait_ge(s["init"], 2)
            dve.wait_ge(s["bias"], 16)
            for g in range(GROUPS):
                dve.wait_ge(loaded[g % 2], 32 * (g // 2 + 1))
                dve.tensor_tensor(ab[:, g % 2], ab[:, g % 2], ab_bias[:].unsqueeze(1).broadcast_to([P, C, 2 * H]),
                                  ALU.add).then_inc(s["biased"], 1)
                heads(dve, "chain", g, 0, HV, count)
                dve.nop().then_inc(s["ready"], 1)
                dve.wait_ge(s["pready"], g + 1)

        @block.gpsimd
        def _(pool):
            count = [0]
            pool.wait_ge(s["init"], 2)
            for g in range(GROUPS):
                pool.wait_ge(loaded[g % 2], 32 * (g // 2 + 1))
                heads(pool, "pchain", g, HV, H, count)
                pool.nop().then_inc(s["pready"], 1)
                pool.wait_ge(s["ready"], g + 1)


def recur(nc, c, d):
    with Stage(nc) as ctx:
        def sb(name, shape, dt=F32):
            return ctx.enter_context(nc.sbuf_tensor("c_" + name, shape, dt))

        def pb(name, shape):
            return ctx.enter_context(nc.psum_tensor("c_" + name, shape, F32))

        BH = B // 2
        kv_in = sb("kv_in", [P, 2, 2, H, HD])
        inv_in = sb("inv_in", [P, 2, INV_COLS])
        q_in = sb("q_in", [P, 2, H, HD])
        g_in = sb("g_in", [P, 2, H])
        ka = sb("ka", [P, 2, 2, H * HD])
        kv = sb("kv", [P, 2, H, QUAD])
        gq = sb("gq", [P, 2, HPQ, NQ, QUAD])
        tbd = sb("tbd", [P, 2, B, H, C])
        kabd = sb("kabd", [P, 2, B, 2, H, HD])
        w_sb = sb("w_sb", [P, NQ, P])
        wu = sb("wu", [P, 2, NQ, NQ, QUAD])
        y_sb = sb("y_sb", [P, 2, HPQ, B, QUAD])
        ybd = sb("ybd", [P, 2, NQ, HPQ, B, QUAD])
        yt = sb("yt", [P, 2, HPQ, B, QUAD])
        s_sb = sb("s_sb", [P, B, P])
        state = sb("state", [P, 2, B, HPQ, HD])
        tmp = sb("tmp", [P, B, HPQ, HD])
        end_decay = sb("end_decay", [P, TILES, B * HPQ])
        ps_w, ps_wt = pb("ps_w", [P, NQ, P]), pb("ps_wt", [P, NQ, P])
        ps_y, ps_s, ps_st = pb("ps_y", [P, HPQ, B, QUAD]), pb("ps_s", [P, B, P]), pb("ps_st", [P, B, P])
        names = ["a_in0", "a_in1", "b_in0", "b_in1", "clear", "clear_end", "clear_y", "end", "tmpa", "tmp", "kv", "kd", "gq", "tbd", "kab_v",
                 "kab_s", "w", "wsb", "wt", "wu", "y", "ysb", "yt", "ybd0", "ybd1", "seq0", "seq1", "ss0", "ss1",
                 "st0", "st1", "s0", "s1", "out0", "out1"]
        s = {n: ctx.semaphore("c_" + n) for n in names}
        tok_t = d["tok"].rearrange("(c p) n -> p c n", p=P)
        inv_t = d["inv"].rearrange("(c b) (j n) -> c j b n", b=B, j=C)
        att_t = d["att"].rearrange("(c b) (j n) -> c j b n", b=B, j=C)
        o_t = d["o"].rearrange("c p n -> p c n")
        KAV = 5
        FIRST, PEEL, END = -5, 2, TILES
        block = ctx.enter_context(nc.Block())

        @block.sync
        def _(sp):
            sk = Skew(sp, TILES)
            sp.wait_ge(s["clear_end"], 1)
            for q in range(NQ):
                sp.dma_start(end_decay[q * QUAD:q * QUAD + HD],
                             d["end"][q].partition_broadcast(HD)).then_inc(s["end"], 16)

            def load_a(t):
                at_least(sp, s["kv"], t.j - 1)
                at_least(sp, s["kd"], t.j - 1)
                at_least(sp, s["tbd"], t.j - 1)
                sp.dma_start(kv_in[:, t.p:t.p + 1].rearrange("p a n h e -> p a (n h e)"),
                             tok_t[:, tile_rows(t), D:3 * D]).then_inc(s[f"a_in{t.p}"], 16)
                sp.dma_start(inv_in[:, t.p], inv_t[tile_rows(t)].rearrange("c j b n -> (c j) b n")).then_inc(s[f"a_in{t.p}"], 16)

            def load_b(t):
                at_least(sp, s["kab_v"], t.j - 1)
                at_least(sp, s["kab_s"], t.j - 1)
                at_least(sp, s["gq"], t.j - 1)
                rows = att_t[tile_rows(t)].rearrange("c j b n -> (c j) b n")
                sp.dma_start(g_in[:, t.p], rows[:, :, H * C:ATT_COLS]).then_inc(s[f"b_in{t.p}"], 16)
                sp.dma_start(q_in[:, t.p:t.p + 1].rearrange("p a h e -> p a (h e)"),
                             tok_t[:, tile_rows(t), 0:D]).then_inc(s[f"b_in{t.p}"], 16)
                sp.dma_start(ka[:, t.p, 1], rows[:, :, 0:H * C]).then_inc(s[f"b_in{t.p}"], 16)

            def spread_y(t):
                sp.wait_ge(s["ysb"], t.j + 1)
                sp.wait_ge(s["clear_y"], 1)
                at_least(sp, s["seq0"], t.j - 1)
                at_least(sp, s["seq1"], t.j - 1)
                for q in range(NQ):
                    rows = slice(q * QUAD, q * QUAD + HD)
                    sp.dma_start(ybd[rows, t.p, q], y_sb[rows, t.p]).then_inc(s[f"ybd{t.p}"], 16)

            def store(t):
                sp.wait_ge(s["s0"], t.j + 2)
                sp.wait_ge(s["s1"], t.j + 2)
                sp.dma_start(o_t[:, tile_rows(t)], state[:, 1 - t.p:2 - t.p].rearrange("p a b q e -> p a (b q e)")
                             ).then_inc(s[f"out{t.p}"], 16)

            def iteration(t):
                sk.do(load_b, t.plus(4))
                sk.do(load_a, t.plus(5))
                sk.do(store, t.plus(-1))
                sk.do(spread_y, t.plus(2))

            sk.run(iteration, FIRST, PEEL, END + 1)
            for p in range(2):
                sp.wait_ge(s[f"out{p}"], 16 * (TILES // 2))

        @block.tensor
        def _(pe):
            sk = Skew(pe, TILES)
            pe.wait_ge(s["clear"], 1)

            def solve(t):
                pe.wait_ge(s["kv"], t.j + 1)
                pe.wait_ge(s["tbd"], t.j + 1)
                at_least(pe, s["wsb"], t.j)
                for m in range(HPQ):
                    for q in range(NQ):
                        h = HPQ * q + m
                        last = pe.matmul(ps_w[q * QUAD:(q + 1) * QUAD, m], kv[:, t.p, h], tbd[:, t.p, :, h].rearrange("p b t -> p t b"),
                                         start=True, stop=True)
                last.then_inc(s["w"], 1)

            def solve_t(t):
                pe.wait_ge(s["wsb"], t.j + 1)
                at_least(pe, s["wu"], t.j)
                for m in range(HPQ):
                    last = pe.transpose(ps_wt[:, m], w_sb[:, m], c["ident"][:])
                last.then_inc(s["wt"], 1)

            def chunk(t):
                pe.wait_ge(s["wu"], t.j + 1)
                pe.wait_ge(s["gq"], t.j + 1)
                pe.wait_ge(s["kab_v"], t.j + 1)
                pe.wait_ge(s["kab_s"], t.j + 1)
                at_least(pe, s["ysb"], t.j)
                for m in range(HPQ):
                    pe.matmul(ps_y[:, m, :, HD:QUAD], gq[:, t.p, m].rearrange("p q x -> p (q x)"),
                              c["ident"][:].rearrange("p (t b) -> p b t", b=B), start=(m % 2 == 0), stop=False,
                              skip_group_check=True)
                    for q in range(NQ):
                        h = HPQ * q + m
                        last = pe.matmul(ps_y[q * QUAD:(q + 1) * QUAD, m], wu[:, t.p, m, q],
                                         kabd[:, t.p, :, :, h], start=False, stop=True, skip_group_check=True)
                last.then_inc(s["y"], 1)

            def advance(t, half):
                pe.wait_ge(s[f"s{half}"], t.j + 1)
                pe.wait_ge(s[f"ybd{t.p}"], (t.half + 1) * 16 * NQ)
                at_least(pe, s[f"ss{half}"], t.j)
                for b in range(half * BH, (half + 1) * BH):
                    for m in range(HPQ):
                        last = pe.matmul(ps_s[m * QUAD:m * QUAD + HD, b], state[:, t.p, b, m],
                                         ybd[:, t.p, :, m, b], start=True, stop=True)
                last.then_inc(s[f"seq{half}"], 1)

            def advance_t(t, half):
                pe.wait_ge(s[f"ss{half}"], t.j + 1)
                for b in range(half * BH, (half + 1) * BH):
                    last = pe.transpose(ps_st[:, b], s_sb[:, b], c["ident"][:])
                last.then_inc(s[f"st{half}"], 1)

            def iteration(t):
                sk.do(lambda u: advance(u, 0), t)
                sk.do(lambda u: advance(u, 1), t)
                sk.do(solve, t.plus(3))
                sk.do(lambda u: advance_t(u, 0), t)
                sk.do(lambda u: advance_t(u, 1), t)
                sk.do(solve_t, t.plus(3))
                sk.do(chunk, t.plus(2))

            sk.run(iteration, FIRST, PEEL, END)

        @block.scalar
        def _(act):
            sk = Skew(act, TILES)
            act.wait_ge(s["clear"], 1)

            def copy_s(t, half):
                act.wait_ge(s[f"seq{half}"], t.j + 1)
                at_least(act, s[f"st{half}"], t.j)
                bs = slice(half * BH, (half + 1) * BH)
                act.activation(s_sb[:, bs], ps_s[:, bs], ACT.Copy).then_inc(s[f"ss{half}"], 1)

            def copy_w(t):
                act.wait_ge(s["w"], t.j + 1)
                at_least(act, s["wt"], t.j)
                act.activation(w_sb[:], ps_w[:], ACT.Copy).then_inc(s["wsb"], 1)

            def copy_wu(t):
                act.wait_ge(s["wt"], t.j + 1)
                at_least(act, s["y"], t.j - 1)
                act.activation(wu[:, t.p].rearrange("p m q x -> p m (q x)"), ps_wt[:], ACT.Copy).then_inc(s["wu"], 1)

            def copy_y(t):
                act.wait_ge(s["y"], t.j + 1)
                at_least(act, s["yt"], t.j - 1)
                at_least(act, s[f"ybd{t.p}"], t.half * 16 * NQ)
                act.activation(y_sb[:, t.p], ps_y[:], ACT.Copy).then_inc(s["ysb"], 1)

            def spread_ka(t):
                act.wait_ge(s["kd"], t.j + 1)
                act.wait_ge(s[f"b_in{t.p}"], (t.half + 1) * 48)
                at_least(act, s["y"], t.j - 1)
                for b in range(KAV, B):
                    last = act.activation(kabd[:, t.p, b].rearrange("p n h e -> p (n h e)"),
                                          ka[:, t.p].rearrange("p n x -> p (n x)"), ACT.Copy,
                                          scale=c["mask_b"][:, b:b + 1])
                last.then_inc(s["kab_s"], 1)

            def iteration(t):
                sk.do(lambda u: copy_s(u, 0), t)
                sk.do(lambda u: copy_s(u, 1), t)
                sk.do(copy_w, t.plus(3))
                sk.do(spread_ka, t.plus(3))
                sk.do(copy_wu, t.plus(3))
                sk.do(copy_y, t.plus(2))

            sk.run(iteration, FIRST, PEEL, END)

        @block.vector
        def _(dve):
            sk = Skew(dve, TILES)
            dve.memset(end_decay[:], 0.0).then_inc(s["clear_end"], 1)
            dve.memset(gq[:], 0.0)
            dve.memset(ps_s[:], 0.0)
            dve.memset(state[:, 0], 0.0).then_inc(s["clear"], 1)
            dve.wait_ge(s["clear"], 1)
            for half in range(2):
                dve.nop().then_inc(s[f"s{half}"], 1)

            def spread_inv(t):
                dve.wait_ge(s[f"a_in{t.p}"], (t.half + 1) * 32)
                at_least(dve, s["w"], t.j - 1)
                for b in range(B):
                    last = dve.tensor_scalar(tbd[:, t.p, b].rearrange("p h t -> p (h t)"), inv_in[:, t.p, 0:H * C],
                                             c["mask_b"][:, b:b + 1], None, ALU.mult)
                last.then_inc(s["tbd"], 1)

            def spread_ka(t):
                dve.wait_ge(s["kd"], t.j + 1)
                dve.wait_ge(s[f"b_in{t.p}"], (t.half + 1) * 48)
                at_least(dve, s["y"], t.j - 1)
                for b in range(KAV):
                    last = dve.tensor_scalar(kabd[:, t.p, b].rearrange("p n h e -> p (n h e)"),
                                             ka[:, t.p].rearrange("p n x -> p (n x)"),
                                             c["mask_b"][:, b:b + 1], None, ALU.mult)
                last.then_inc(s["kab_v"], 1)

            def next_state(t, half):
                dve.wait_ge(s[f"st{half}"], t.j + 1)
                dve.wait_ge(s["tmp"], t.j + 1)
                at_least(dve, s[f"out{t.p}"], t.half * 16)
                bs = slice(half * BH, (half + 1) * BH)
                dve.tensor_tensor(state[:, 1 - t.p, bs], ps_st[:, bs].rearrange("p b (m x) -> p b m x", m=HPQ)[:, :, :, 0:HD],
                                  tmp[:, bs], ALU.add).then_inc(s[f"s{half}"], 1)

            def turn_y(t):
                dve.wait_ge(s["ysb"], t.j + 1)
                at_least(dve, s["tmp"], t.j - 1)
                dve.transpose(yt[:, t.p].rearrange("p m b x -> p (m b x)"),
                              y_sb[:, t.p].rearrange("p m b x -> p (m b x)")).then_inc(s["yt"], 1)

            def iteration(t):
                sk.do(spread_ka, t.plus(3))
                sk.do(lambda u: next_state(u, 0), t)
                sk.do(lambda u: next_state(u, 1), t)
                sk.do(spread_inv, t.plus(4))
                sk.do(turn_y, t.plus(2))

            sk.run(iteration, FIRST, PEEL, END)

        @block.gpsimd
        def _(pool):
            sk = Skew(pool, TILES)
            pool.memset(ybd[:], 0.0).then_inc(s["clear_y"], 1)
            pool.wait_ge(s["clear"], 1)
            pool.wait_ge(s["end"], 16 * NQ)

            def carry(t):
                pool.wait_ge(s["s0"], t.j + 1)
                pool.wait_ge(s["s1"], t.j + 1)
                pool.tensor_tensor(tmp[:].rearrange("p b m e -> p (b m) e"), state[:, t.p].rearrange("p b m e -> p (b m) e"),
                                   end_decay[:, tile_rows(t)].rearrange("p a n -> p (a n)").unsqueeze(2)
                                   .broadcast_to([P, B * HPQ, HD]), ALU.mult).then_inc(s["tmpa"], 1)
                pool.wait_ge(s["tmpa"], t.j + 1)
                pool.wait_ge(s["yt"], t.j + 1)
                pool.tensor_tensor(tmp[:], tmp[:], yt[:, t.p].rearrange("p m b x -> p b m x")[:, :, :, HD:QUAD],
                                   ALU.add).then_inc(s["tmp"], 1)

            def scale(dst, src, factor):
                return pool.tensor_tensor(dst, src, factor.unsqueeze(2).broadcast_to([P, H, HD]), ALU.mult)

            def token_scale(t):
                pool.wait_ge(s[f"a_in{t.p}"], (t.half + 1) * 32)
                at_least(pool, s["w"], t.j - 1)
                sc = inv_in[:, t.p, H * C:INV_COLS]
                scale(kv[:, t.p, :, 0:HD], kv_in[:, t.p, 0], sc[:, 0:H])
                scale(kv[:, t.p, :, HD:QUAD], kv_in[:, t.p, 1], sc[:, 3 * H:4 * H]).then_inc(s["kv"], 1)
                at_least(pool, s["kab_v"], t.j - 1)
                at_least(pool, s["kab_s"], t.j - 1)
                scale(ka[:, t.p, 0].rearrange("p (h e) -> p h e", h=H), kv_in[:, t.p, 0],
                      sc[:, 2 * H:3 * H]).then_inc(s["kd"], 1)

            def query_scale(t):
                pool.wait_ge(s[f"b_in{t.p}"], (t.half + 1) * 48)
                at_least(pool, s["y"], t.j - 1)
                pool.tensor_tensor(gq[:, t.p].rearrange("p m q x -> p q m x")[:, :, :, 0:HD],
                                   q_in[:, t.p].rearrange("p (q m) e -> p q m e", m=HPQ),
                                   g_in[:, t.p].rearrange("p (q m) -> p q m", m=HPQ).unsqueeze(3)
                                   .broadcast_to([P, NQ, HPQ, HD]), ALU.mult).then_inc(s["gq"], 1)

            def iteration(t):
                sk.do(carry, t)
                sk.do(token_scale, t.plus(4))
                sk.do(query_scale, t.plus(3))

            sk.run(iteration, FIRST, PEEL, END)


def output(nc, x, dst, wo, g_norm, c, d):
    with Stage(nc) as ctx:
        def sb(name, shape, dt=F32):
            return ctx.enter_context(nc.sbuf_tensor("d_" + name, shape, dt))

        raw, gn = sb("raw", [P, KT, D]), sb("gn", [P, KT])
        w_h, w_l = sb("w_h", [P, KT, D], F32R), sb("w_l", [P, KT, D], F32R)
        o_in = sb("o_in", [P, 2, 2, D])
        gate, xt = sb("gate", [P, 2, 2, D]), sb("xt", [P, 2, 2, D])
        sig = sb("sig", [P, 2, D])
        sq, ss, rstd = sb("sq", [P, D]), sb("ss", [P, 2, 2]), sb("rstd", [P, 2, 2])
        y, res = sb("y", [P, 2, 2, D]), sb("res", [P, 2, 2, D])
        y_h, y_l = sb("y_h", [P, 2, KT, P], F32R), sb("y_l", [P, 2, KT, P], F32R)
        ps_t = ctx.enter_context(nc.psum_tensor("d_ps_t", [P, 2, 2, KT, P], F32))
        ps_o = ctx.enter_context(nc.psum_tensor("d_ps_o", [P, 2, 2, D], F32))
        names = ["raw", "wg", "wh", "wl", "in0", "in1", "x0", "x1", "sq", "ms", "rstd", "silu", "y", "yt", "yh", "yl", "o", "sum",
                 "out0", "out1"]
        s = {n: ctx.semaphore("d_" + n) for n in names}
        x_t = x.rearrange("(c p) d -> p c d", p=P)
        out_t = dst.rearrange("(c p) d -> p c d", p=P)
        tok_t = d["tok"].rearrange("(c p) n -> p c n", p=P)
        o_t = d["o"].rearrange("c (q z t) (b m) -> c z (t b) q m", q=NQ, z=2, b=B)
        PAIRS_T = TILES // 2
        IN = 16 * 3
        FIRST, PEEL, END = -4, 4, PAIRS_T + 1
        block = ctx.enter_context(nc.Block())

        def two(t):
            return bass.ds(t.j * 2, 2)

        @block.sync
        def _(sp):
            sk = Skew(sp, PAIRS_T)
            sp.dma_start(raw[:], wo.rearrange("(k p) n -> p k n", p=P)).then_inc(s["raw"], 16)
            sp.dma_start(gn[:], g_norm).then_inc(s["raw"], 16)

            def load(t):
                at_least(sp, s["y"], t.j - 1)
                for u in range(2):
                    sp.dma_start(o_in[:, t.p, u].rearrange("p (q m) -> p q m", q=NQ),
                                 o_t[bass.ds(t.j * 2 + u, 1), 1].rearrange("c p q m -> (c p) q m")
                                 ).then_inc(s[f"in{t.p}"], 16)
                sp.dma_start(gate[:, t.p], tok_t[:, two(t), 3 * D:4 * D]).then_inc(s[f"in{t.p}"], 16)

            def load_x(t):
                at_least(sp, s["sum"], t.j - 1)
                sp.dma_start(xt[:, t.p], x_t[:, two(t)]).then_inc(s[f"x{t.p}"], 16)

            def store(t):
                sp.wait_ge(s["sum"], t.j + 1)
                sp.dma_start(out_t[:, two(t)], res[:, t.p]).then_inc(s[f"out{t.p}"], 16)

            def iteration(t):
                sk.do(load, t.plus(4))
                sk.do(load_x, t.plus(1))
                sk.do(store, t.plus(-1))

            sk.run(iteration, FIRST, PEEL, END)
            for p in range(2):
                sp.wait_ge(s[f"out{p}"], 16 * (PAIRS_T // 2))

        @block.scalar
        def _(act):
            sk = Skew(act, PAIRS_T)
            act.wait_ge(s["wg"], 1)
            act.activation(w_h[:], raw[:], ACT.Copy).then_inc(s["wh"], 1)

            def squares(t):
                act.wait_ge(s[f"in{t.p}"], (t.half + 1) * IN)
                at_least(act, s["rstd"], t.j - 1)
                at_least(act, s["y"], t.j)
                for u in range(2):
                    if u:
                        act.wait_ge(s["sq"], t.j * 2 + 1)
                    else:
                        at_least(act, s["sq"], t.j * 2)
                    act.activation(sq[:], o_in[:, t.p, u], ACT.Square,
                                   accum_out=ss[:, t.p, u:u + 1]).then_inc(s["sq"], 1)
                act.activation(sig[:], gate[:, t.p], ACT.Silu).then_inc(s["silu"], 1)

            def high(t):
                act.wait_ge(s["yt"], t.j + 1)
                at_least(act, s["o"], t.j)
                act.activation(y_h[:], ps_t[:, t.p], ACT.Copy).then_inc(s["yh"], 1)

            def iteration(t):
                sk.do(high, t)
                sk.do(squares, t.plus(2))

            sk.run(iteration, FIRST, PEEL, END)

        @block.gpsimd
        def _(pool):
            sk = Skew(pool, PAIRS_T)

            def power(t):
                pool.wait_ge(s["ms"], t.j + 1)
                at_least(pool, s["sum"], t.j - 1)
                pool.tensor_tensor(rstd[:, t.p], ss[:, t.p], c["minus_half"][:], ALU.pow).then_inc(s["rstd"], 1)

            sk.run(lambda t: sk.do(power, t.plus(2)), FIRST, PEEL, END)

        @block.vector
        def _(dve):
            sk = Skew(dve, PAIRS_T)
            dve.memset(ss[:], 0.0)
            dve.wait_ge(s["raw"], 32)
            for k in range(KT):
                last = dve.tensor_scalar(raw[:, k], raw[:, k], gn[:, k:k + 1], None, ALU.mult)
            last.then_inc(s["wg"], 1)
            dve.wait_ge(s["wh"], 1)
            dve.tensor_tensor(w_l[:], raw[:], w_h[:].bitcast(F32), ALU.subtract).then_inc(s["wl"], 1)

            def gated(t):
                dve.wait_ge(s["sq"], t.j * 2 + 2)
                dve.tensor_scalar(ss[:, t.p], ss[:, t.p], 1.0 / D, EPS, ALU.mult, ALU.add).then_inc(s["ms"], 1)
                dve.wait_ge(s["silu"], t.j + 1)
                at_least(dve, s["yt"], t.j - 1)
                dve.tensor_tensor(y[:, t.p], o_in[:, t.p], sig[:], ALU.mult).then_inc(s["y"], 1)

            def low(t):
                dve.wait_ge(s["yh"], t.j + 1)
                at_least(dve, s["o"], t.j)
                dve.tensor_tensor(y_l[:], ps_t[:, t.p], y_h[:].bitcast(F32), ALU.subtract).then_inc(s["yl"], 1)

            def add(t):
                dve.wait_ge(s["o"], t.j + 1)
                dve.wait_ge(s["rstd"], t.j + 1)
                dve.wait_ge(s[f"x{t.p}"], (t.half + 1) * 16)
                at_least(dve, s[f"out{t.p}"], t.half * 16)
                for u in range(2):
                    last = dve.scalar_tensor_tensor(res[:, t.p, u], ps_o[:, t.p, u], rstd[:, t.p, u:u + 1], xt[:, t.p, u],
                                                    ALU.mult, ALU.add)
                last.then_inc(s["sum"], 1)

            def iteration(t):
                sk.do(low, t)
                sk.do(gated, t.plus(2))
                sk.do(add, t.plus(-1))

            sk.run(iteration, FIRST, PEEL, END)

        @block.tensor
        def _(pe):
            sk = Skew(pe, PAIRS_T)
            pe.wait_ge(s["wl"], 1)

            def turn(t):
                pe.wait_ge(s["y"], t.j + 1)
                at_least(pe, s["yl"], t.j - 1)
                for u in range(2):
                    for k in range(KT):
                        last = pe.transpose(ps_t[:, t.p, u, k], y[:, t.p, u, k * P:(k + 1) * P], c["ident"][:])
                last.then_inc(s["yt"], 1)

            def product(t):
                pe.wait_ge(s["yh"], t.j + 1)
                pe.wait_ge(s["yl"], t.j + 1)
                at_least(pe, s["sum"], t.j - 1)
                for u in range(2):
                    m = 0
                    for yy, ww in ((y_h, w_h), (y_h, w_l), (y_l, w_h)):
                        for k in range(KT):
                            last = pe.matmul(ps_o[:, t.p, u], yy[:, u, k], ww[:, k], start=(m == 0), stop=(m == 5))
                            m += 1
                last.then_inc(s["o"], 1)

            def iteration(t):
                sk.do(product, t)
                sk.do(turn, t.plus(1))

            sk.run(iteration, FIRST, PEEL, END)


CONSTANTS = {
    "ident": ([P, P], lambda: np.eye(P)),
    "before": ([P, P], lambda: np.triu(np.ones((P, P)), 1)),
    "ones": ([P, P], lambda: np.ones((P, P))),
    "iota_e": ([P, E], lambda: np.tile(np.arange(E), (P, 1))),
    "iota_128": ([P, PAIRS], lambda: np.tile(np.arange(PAIRS) * P, (P, 1))),
    "iota_tile": ([1, SLOT_TILES], lambda: np.arange(SLOT_TILES)[None]),
    "dump_row": ([P, PAIRS], lambda: SLOTS + np.arange(PAIRS)[None] * P + np.arange(P)[:, None]),
    "eps": ([P, 1], lambda: np.full((P, 1), EPS)),
    "minus_half": ([P, 2], lambda: np.full((P, 2), -0.5)),
    "mask_b": ([P, B], lambda: np.arange(P)[:, None] % B == np.arange(B)[None]),
    "mask16": ([P, HALF], lambda: np.arange(P)[:, None] // HD == np.arange(HALF)[None]),
}


def layer(nc, t, out):
    with Stage(nc) as ctx:
        def dram(name, shape):
            return nc.dram_tensor(name, shape, F32, kind="Internal").ap()

        x = t["x"]
        x1 = dram("x_after_first", [SEQ * BATCHES, D])
        slots = dict(xs=dram("slot_rows", [SLOTS + DUMP, D]), ys=dram("slot_results", [SLOTS, D]))
        scratch = dict(tok=dram("projections", [SEQ * BATCHES, 4 * D]), ab=dram("decay_logits", [SEQ * BATCHES, 2 * H]),
                       gram=dram("chunk_products", [TILES, 2 * B * C, H * C]),
                       inv=dram("inverses", [TILES * B, C * INV_COLS]), att=dram("masked_qk", [TILES * B, C * ATT_COLS]),
                       end=dram("end_decays", [NQ, TILES, B * HPQ]), o=dram("states", [TILES, P, B * D // NQ]))
        consts = {k: ctx.enter_context(nc.sbuf_tensor(f"const_{k}_sb", shape, F32)) for k, (shape, _) in CONSTANTS.items()}
        slots["pos_gather"] = ctx.enter_context(nc.sbuf_tensor("pos_gather", [P, PAIRS], I32))
        slots["pos_scatter"] = ctx.enter_context(nc.sbuf_tensor("pos_scatter", [P, PAIRS], I32))
        slots["half_w"] = ctx.enter_context(nc.sbuf_tensor("half_w", [P, PAIRS], F32))
        slots["tile_expert"] = ctx.enter_context(nc.sbuf_tensor("tile_expert", [1, SLOT_TILES], I32))
        copied = ctx.semaphore("rest_copied")
        consts_in = ctx.semaphore("consts_in")
        with nc.Block() as block:
            @block.sync
            def _(sp):
                for k in consts:
                    sp.dma_start(consts[k][:], t["const_" + k]).then_inc(consts_in, 16)
                sp.dma_start(x1.rearrange("(n b) d -> n b d", b=B)[:, FFN_BATCHES:B],
                             x.rearrange("(n b) d -> n b d", b=B)[:, FFN_BATCHES:B]).then_inc(copied, 16)
                sp.wait_ge(consts_in, 16 * len(consts))

        expert_w = (t["w1a_t"], t["w1b"], t["w2a_t"], t["w2b"])
        routing(nc, t["expert_indices"], t["expert_weights"], consts, slots)
        ffn_experts(nc, "fe1", x, expert_w, consts, slots)
        ffn_combine(nc, "fc1", x, x1, consts, slots)
        with nc.Block() as block:
            @block.sync
            def _(sp):
                sp.wait_ge(copied, 16)

        project(nc, x1, [t[n] for n in ("wk", "wq", "wv", "wg", "wa", "wb")], consts, scratch)
        solve_chunks(nc, t["gate_bias"], consts, scratch)
        recur(nc, consts, scratch)
        output(nc, x1, out, t["wo"], t["g_norm"], consts, scratch)
        ffn_experts(nc, "fe2", out, expert_w, consts, slots)
        ffn_combine(nc, "fc2", out, out, consts, slots)


def kernel(L0_attn_x, L0_attn_Wq, L0_attn_Wk, L0_attn_Wv, L0_attn_Wa, L0_attn_ba, L0_attn_Wb, L0_attn_bb, L0_attn_Wg,
           L0_attn_Wo, L0_attn_g_norm, L0_ffn_expert_weights, L0_ffn_expert_indices, L0_ffn_w1_A, L0_ffn_w1_B,
           L0_ffn_w2_A, L0_ffn_w2_B):
    import concourse.bacc as bacc
    from concourse.bass_utils import run_bass_kernel_spmd

    def in_tiles(a, batches):
        a = np.asarray(a)
        return a.reshape(batches, SEQ, a.shape[-1]).transpose(1, 0, 2).reshape(batches * SEQ, a.shape[-1])

    arrays = {
        "x": in_tiles(L0_attn_x, BATCHES),
        "wk": L0_attn_Wk, "wq": L0_attn_Wq, "wv": L0_attn_Wv, "wg": L0_attn_Wg, "wa": L0_attn_Wa, "wb": L0_attn_Wb,
        "gate_bias": np.concatenate([np.asarray(L0_attn_ba), np.asarray(L0_attn_bb)]),
        "wo": L0_attn_Wo, "g_norm": np.asarray(L0_attn_g_norm).reshape(KT, P).T,
        "expert_weights": in_tiles(L0_ffn_expert_weights, FFN_BATCHES),
        "expert_indices": in_tiles(L0_ffn_expert_indices, FFN_BATCHES),
        "w1a_t": np.asarray(L0_ffn_w1_A).T, "w1b": L0_ffn_w1_B, "w2a_t": np.asarray(L0_ffn_w2_A).T, "w2b": L0_ffn_w2_B,
    }
    for name, (_, value) in CONSTANTS.items():
        arrays["const_" + name] = value().astype(np.float32)
    arrays = {name: np.ascontiguousarray(a) for name, a in arrays.items()}
    nc = bacc.Bacc("TRN2", target_bir_lowering=False, num_devices=1)
    tensors = {name: nc.dram_tensor(name, a.shape, mybir.dt.from_np(a.dtype), kind="ExternalInput").ap()
               for name, a in arrays.items()}
    out = nc.dram_tensor("out", (SEQ * BATCHES, D), F32, kind="ExternalOutput").ap()
    layer(nc, tensors, out)
    result = run_bass_kernel_spmd(nc, [arrays], core_ids=[0]).results[0]["out"]
    return result.reshape(SEQ, BATCHES, D).transpose(1, 0, 2)
```
